# Optimizing a Trainium2 kernel written in Bass

```python
import numpy as np
import jax
import jax.numpy as jnp

def _softmax(x, axis=-1):
    return jax.nn.softmax(x, axis=axis)

def _gelu(x):
    return jax.nn.gelu(x, approximate=True)

def _silu(x):
    return jax.nn.silu(x)

def _sigmoid(x):
    return jax.nn.sigmoid(x)

def _layernorm(x, axis=-1, eps=1e-05):
    m = jnp.mean(x, axis=axis, keepdims=True)
    v = jnp.var(x, axis=axis, keepdims=True)
    return (x - m) / jnp.sqrt(v + eps)

def _scatter_add(tgt, idx, src, axis=0):
    return tgt.at[idx].add(src)

def _segment_sum(src, seg, n):
    return jax.ops.segment_sum(src, seg, n)
kernel_name = 'mk_macaron_d2_jaxref_r8_9b4be4'

def setup_inputs(seed: int=0):
    np.random.seed(seed)
    _w = jnp.asarray

    def _L0_attn_setup():
        import jax, jax.numpy as jnp
        import numpy as np
        BSZ, T, DM, N = (8, 512, 128, 64)
        LN_EPS = 1e-05
        key = jax.random.key(seed)
        ks = jax.random.split(key, 7)
        return {'x': jax.random.normal(ks[0], (BSZ, T, DM), jnp.float32), 'log_A': jax.random.normal(ks[1], (DM, N), jnp.float32) * 0.01 - 4.0, 'B_param': jax.random.normal(ks[2], (DM, N), jnp.float32) * 0.01, 'C_param': jax.random.normal(ks[3], (DM, N), jnp.float32) * 0.01, 'D_param': jnp.ones((DM,), jnp.float32), 'log_dt': jax.random.normal(ks[4], (DM,), jnp.float32) * 0.01 - 4.0, 'ln_gamma': jnp.ones((DM,), jnp.float32), 'ln_beta': jnp.zeros((DM,), jnp.float32), 'W_out': jax.random.normal(ks[5], (DM, DM), jnp.float32) / np.sqrt(DM).astype(np.float32), 'b_out': jnp.zeros((DM,), jnp.float32)}
    _L0_attn_in = _L0_attn_setup()

    def _L0_ffn_setup():
        import jax, jax.numpy as jnp
        import numpy as np
        DIM = 128
        DEPTH = 2
        HEADS = 8
        DIM_HEAD = 64
        WINDOW = 64
        INNER = HEADS * DIM_HEAD
        HID = int(DIM * 4 * 2 / 3)
        B, N = (2, 1024)
        QK_SCALE = 8.0

        def shift_token(t):
            t1, t2 = jnp.split(t, 2, axis=-1)
            t2 = jnp.pad(t2, ((0, 0), (1, 0), (0, 0)))[:, :-1]
            return jnp.concatenate([t1, t2], axis=-1)

        def l2norm(t):
            return t / jnp.clip(jnp.linalg.norm(t, axis=-1, keepdims=True), 1e-12)

        def rotate_half(x):
            x1, x2 = jnp.split(x, 2, axis=-1)
            return jnp.concatenate([-x2, x1], axis=-1)

        def rotary_xpos(q, k):
            n = q.shape[-2]
            half_idx = jnp.arange(0, DIM_HEAD, 2, dtype=jnp.float32)
            inv_freq = 1.0 / 10000.0 ** (half_idx / DIM_HEAD)
            t = jnp.arange(n, dtype=jnp.float32)
            freqs = t[:, None] * inv_freq[None, :]
            freqs = jnp.concatenate([freqs, freqs], axis=-1)
            base = (half_idx + 0.4 * DIM_HEAD) / (1.4 * DIM_HEAD)
            power = (t - n // 2) / float(WINDOW // 2)
            scale = base[None, :] ** power[:, None]
            scale = jnp.concatenate([scale, scale], axis=-1)
            cos, sin = (jnp.cos(freqs), jnp.sin(freqs))
            q = q * cos * scale + rotate_half(q) * sin * scale
            k = k * cos / scale + rotate_half(k) * sin / scale
            return (q, k)

        def local_attention(q, k, v):
            b, h, n, d = q.shape
            w = n // WINDOW
            bq = q.reshape(b, h, w, WINDOW, d) * QK_SCALE
            bk = k.reshape(b, h, w, WINDOW, d)
            bv = v.reshape(b, h, w, WINDOW, d)

            def look_around(t):
                p = jnp.pad(t, ((0, 0), (0, 0), (1, 0), (0, 0), (0, 0)))
                return jnp.concatenate([p[:, :, :w], p[:, :, 1:]], axis=3)
            bk, bv = (look_around(bk), look_around(bv))
            bt = jnp.arange(n).reshape(w, WINDOW)
            btp = jnp.pad(bt, ((1, 0), (0, 0)), constant_values=-1)
            btk = jnp.concatenate([btp[:w], btp[1:]], axis=1)
            sim = jnp.einsum('bhwid,bhwjd->bhwij', bq, bk)
            i = bt[:, :, None]
            j = btk[:, None, :]
            mask = (i < j) | (i > j + WINDOW) | (j == -1)
            sim = jnp.where(mask, -jnp.finfo(sim.dtype).max, sim)
            attn = jax.nn.softmax(sim, axis=-1)
            out = jnp.einsum('bhwij,bhwjd->bhwid', attn, bv)
            return out.reshape(b, h, n, d)

        def _layer(x, wqkv, qs, ksc, wo, lg, lb, w1, b1, w2, b2):
            b, n, _ = x.shape
            h = shift_token(x)
            qkv = h @ wqkv
            q, k, v = jnp.split(qkv, 3, axis=-1)
            to_heads = lambda t: t.reshape(b, n, HEADS, DIM_HEAD).transpose(0, 2, 1, 3)
            q, k, v = (to_heads(q), to_heads(k), to_heads(v))
            q = l2norm(q) * qs
            k = l2norm(k) * ksc
            q, k = rotary_xpos(q, k)
            o = local_attention(q, k, v)
            o = o.transpose(0, 2, 1, 3).reshape(b, n, INNER)
            x = x + o @ wo
            h = shift_token(x)
            mu = h.mean(-1, keepdims=True)
            var = h.var(-1, keepdims=True)
            h = (h - mu) / jnp.sqrt(var + 1e-05) * lg + lb
            h = h @ w1 + b1
            a, g = jnp.split(h, 2, axis=-1)
            h = a * jax.nn.gelu(g, approximate=False)
            x = x + h @ w2 + b2
            return x
        key = jax.random.key(seed)
        ks = jax.random.split(key, 6)
        return {'x': jax.random.normal(ks[0], (B, N, DIM), jnp.float32), 'wqkv': jax.random.normal(ks[1], (DEPTH, DIM, 3 * INNER), jnp.float32) * 0.02, 'q_scale': jnp.ones((DEPTH, DIM_HEAD), jnp.float32), 'k_scale': jnp.ones((DEPTH, DIM_HEAD), jnp.float32), 'wo': jax.random.normal(ks[2], (DEPTH, INNER, DIM), jnp.float32) * 0.02, 'ln_g': jnp.ones((DEPTH, DIM), jnp.float32), 'ln_b': jnp.zeros((DEPTH, DIM), jnp.float32), 'w1': jax.random.normal(ks[3], (DEPTH, DIM, 2 * HID), jnp.float32) * 0.02, 'b1': jnp.zeros((DEPTH, 2 * HID), jnp.float32), 'w2': jax.random.normal(ks[4], (DEPTH, HID, DIM), jnp.float32) * 0.02, 'b2': jnp.zeros((DEPTH, DIM), jnp.float32)}
    _L0_ffn_in = _L0_ffn_setup()

    def _L1_attn_setup():
        import jax, jax.numpy as jnp
        import numpy as np
        EMBED = 128
        HEADS = 8
        D1 = 256
        HEAD_DIM = D1 // HEADS
        SEQ = 256
        BATCH = 4
        MAXL = 256
        EPS = 1e-08

        def simple_rms_norm(x, d):
            rms = jnp.linalg.norm(x, axis=-1, keepdims=True) * d ** (-0.5)
            return x / (rms + EPS)

        def toeplitz_causal(v, t_zero, t_pos):
            n = v.shape[2]
            t = jnp.concatenate([t_zero, t_pos[:, :n - 1]], axis=-1)
            m = 2 * n
            vf = jnp.fft.rfft(v, m, axis=2)
            tf = jnp.fft.rfft(t, m, axis=-1)
            y = jnp.fft.irfft(vf * tf[None, :, :, None], m, axis=2)
            return y[:, :, :n]
        key = jax.random.key(seed)
        ks = jax.random.split(key, 9)
        s = 0.02
        return {'x': jax.random.normal(ks[0], (SEQ, BATCH, EMBED), jnp.float32), 'u_w': jax.random.normal(ks[1], (D1, EMBED), jnp.float32) * s, 'u_b': jax.random.normal(ks[2], (D1,), jnp.float32) * s, 'v_w': jax.random.normal(ks[3], (D1, EMBED), jnp.float32) * s, 'v_b': jax.random.normal(ks[4], (D1,), jnp.float32) * s, 'o_w': jax.random.normal(ks[5], (EMBED, D1), jnp.float32) * s, 'o_b': jax.random.normal(ks[6], (EMBED,), jnp.float32) * s, 't_zero': jax.random.normal(ks[7], (HEADS, 1), jnp.float32), 't_pos': jax.random.normal(ks[8], (HEADS, MAXL - 1), jnp.float32)}
    _L1_attn_in = _L1_attn_setup()

    def _L1_ffn_setup():
        import jax, jax.numpy as jnp
        import numpy as np
        EMBED_DIM = 128
        HIDDEN_DIM = 512
        NUM_EXPERTS = 8
        TOP_K = 2
        key = jax.random.key(seed)
        ks = jax.random.split(key, 4)
        std1 = float(np.sqrt(2.0 / EMBED_DIM))
        std2 = float(np.sqrt(2.0 / HIDDEN_DIM))
        x = jax.random.normal(ks[0], (1, 256, EMBED_DIM), dtype=jnp.float32)
        w_router = jax.random.normal(ks[1], (EMBED_DIM, NUM_EXPERTS), dtype=jnp.float32) * 0.02
        w1 = jax.random.normal(ks[2], (NUM_EXPERTS, EMBED_DIM, HIDDEN_DIM), dtype=jnp.float32) * std1
        b1 = jnp.zeros((NUM_EXPERTS, HIDDEN_DIM), dtype=jnp.float32)
        w2 = jax.random.normal(ks[3], (NUM_EXPERTS, HIDDEN_DIM, EMBED_DIM), dtype=jnp.float32) * std2
        b2 = jnp.zeros((NUM_EXPERTS, EMBED_DIM), dtype=jnp.float32)
        return {'x': x, 'w_router': w_router, 'w1': w1, 'b1': b1, 'w2': w2, 'b2': b2}
    _L1_ffn_in = _L1_ffn_setup()
    _d = {'L0_attn_x': _L0_attn_in['x'], 'L0_attn_log_A': _L0_attn_in['log_A'], 'L0_attn_B_param': _L0_attn_in['B_param'], 'L0_attn_C_param': _L0_attn_in['C_param'], 'L0_attn_D_param': _L0_attn_in['D_param'], 'L0_attn_log_dt': _L0_attn_in['log_dt'], 'L0_attn_ln_gamma': _L0_attn_in['ln_gamma'], 'L0_attn_ln_beta': _L0_attn_in['ln_beta'], 'L0_attn_W_out': _L0_attn_in['W_out'], 'L0_attn_b_out': _L0_attn_in['b_out'], 'L0_ffn_wqkv': _L0_ffn_in['wqkv'], 'L0_ffn_q_scale': _L0_ffn_in['q_scale'], 'L0_ffn_k_scale': _L0_ffn_in['k_scale'], 'L0_ffn_wo': _L0_ffn_in['wo'], 'L0_ffn_ln_g': _L0_ffn_in['ln_g'], 'L0_ffn_ln_b': _L0_ffn_in['ln_b'], 'L0_ffn_w1': _L0_ffn_in['w1'], 'L0_ffn_b1': _L0_ffn_in['b1'], 'L0_ffn_w2': _L0_ffn_in['w2'], 'L0_ffn_b2': _L0_ffn_in['b2'], 'L1_attn_u_w': _L1_attn_in['u_w'], 'L1_attn_u_b': _L1_attn_in['u_b'], 'L1_attn_v_w': _L1_attn_in['v_w'], 'L1_attn_v_b': _L1_attn_in['v_b'], 'L1_attn_o_w': _L1_attn_in['o_w'], 'L1_attn_o_b': _L1_attn_in['o_b'], 'L1_attn_t_zero': _L1_attn_in['t_zero'], 'L1_attn_t_pos': _L1_attn_in['t_pos'], 'L1_ffn_w_router': _L1_ffn_in['w_router'], 'L1_ffn_w1': _L1_ffn_in['w1'], 'L1_ffn_b1': _L1_ffn_in['b1'], 'L1_ffn_w2': _L1_ffn_in['w2'], 'L1_ffn_b2': _L1_ffn_in['b2']}
    _x0 = _d['L0_attn_x']
    _d['L0_attn_x'] = jax.random.normal(jax.random.fold_in(jax.random.key(seed), 1), (1, 2048, 128), dtype=_x0.dtype)
    del _x0
    return _d

def reference(L0_attn_x, L0_attn_log_A, L0_attn_B_param, L0_attn_C_param, L0_attn_D_param, L0_attn_log_dt, L0_attn_ln_gamma, L0_attn_ln_beta, L0_attn_W_out, L0_attn_b_out, L0_ffn_wqkv, L0_ffn_q_scale, L0_ffn_k_scale, L0_ffn_wo, L0_ffn_ln_g, L0_ffn_ln_b, L0_ffn_w1, L0_ffn_b1, L0_ffn_w2, L0_ffn_b2, L1_attn_u_w, L1_attn_u_b, L1_attn_v_w, L1_attn_v_b, L1_attn_o_w, L1_attn_o_b, L1_attn_t_zero, L1_attn_t_pos, L1_ffn_w_router, L1_ffn_w1, L1_ffn_b1, L1_ffn_w2, L1_ffn_b2):

    def _L0_attn_ref(x, log_A, B_param, C_param, D_param, log_dt, ln_gamma, ln_beta, W_out, b_out):
        import jax, jax.numpy as jnp
        import numpy as np
        BSZ, T, DM, N = (8, 512, 128, 64)
        LN_EPS = 1e-05
        residual = x
        mu = jnp.mean(x, axis=-1, keepdims=True)
        var = jnp.mean(jnp.square(x - mu), axis=-1, keepdims=True)
        xn = (x - mu) / jnp.sqrt(var + LN_EPS) * ln_gamma + ln_beta
        dt = jnp.exp(log_dt)
        dA = jnp.exp(-jnp.exp(log_A) * dt[:, None])
        dB = B_param * dt[:, None]

        def step(h, u):
            h = dA * h + dB * u[..., None]
            y = jnp.einsum('dn,bdn->bd', C_param, h) + D_param * u
            return (h, y)
        h0 = jnp.zeros((x.shape[0], x.shape[2], dA.shape[1]), x.dtype)
        _, ys = jax.lax.scan(step, h0, jnp.swapaxes(xn, 0, 1))
        y = jnp.swapaxes(ys, 0, 1)
        y = jnp.einsum('btd,ed->bte', y, W_out) + b_out
        return residual + y

    def _L0_ffn_ref(x, wqkv, q_scale, k_scale, wo, ln_g, ln_b, w1, b1, w2, b2):
        import jax, jax.numpy as jnp
        import numpy as np
        DIM = 128
        DEPTH = 2
        HEADS = 8
        DIM_HEAD = 64
        WINDOW = 64
        INNER = HEADS * DIM_HEAD
        HID = int(DIM * 4 * 2 / 3)
        B, N = (2, 1024)
        QK_SCALE = 8.0

        def shift_token(t):
            t1, t2 = jnp.split(t, 2, axis=-1)
            t2 = jnp.pad(t2, ((0, 0), (1, 0), (0, 0)))[:, :-1]
            return jnp.concatenate([t1, t2], axis=-1)

        def l2norm(t):
            return t / jnp.clip(jnp.linalg.norm(t, axis=-1, keepdims=True), 1e-12)

        def rotate_half(x):
            x1, x2 = jnp.split(x, 2, axis=-1)
            return jnp.concatenate([-x2, x1], axis=-1)

        def rotary_xpos(q, k):
            n = q.shape[-2]
            half_idx = jnp.arange(0, DIM_HEAD, 2, dtype=jnp.float32)
            inv_freq = 1.0 / 10000.0 ** (half_idx / DIM_HEAD)
            t = jnp.arange(n, dtype=jnp.float32)
            freqs = t[:, None] * inv_freq[None, :]
            freqs = jnp.concatenate([freqs, freqs], axis=-1)
            base = (half_idx + 0.4 * DIM_HEAD) / (1.4 * DIM_HEAD)
            power = (t - n // 2) / float(WINDOW // 2)
            scale = base[None, :] ** power[:, None]
            scale = jnp.concatenate([scale, scale], axis=-1)
            cos, sin = (jnp.cos(freqs), jnp.sin(freqs))
            q = q * cos * scale + rotate_half(q) * sin * scale
            k = k * cos / scale + rotate_half(k) * sin / scale
            return (q, k)

        def local_attention(q, k, v):
            b, h, n, d = q.shape
            w = n // WINDOW
            bq = q.reshape(b, h, w, WINDOW, d) * QK_SCALE
            bk = k.reshape(b, h, w, WINDOW, d)
            bv = v.reshape(b, h, w, WINDOW, d)

            def look_around(t):
                p = jnp.pad(t, ((0, 0), (0, 0), (1, 0), (0, 0), (0, 0)))
                return jnp.concatenate([p[:, :, :w], p[:, :, 1:]], axis=3)
            bk, bv = (look_around(bk), look_around(bv))
            bt = jnp.arange(n).reshape(w, WINDOW)
            btp = jnp.pad(bt, ((1, 0), (0, 0)), constant_values=-1)
            btk = jnp.concatenate([btp[:w], btp[1:]], axis=1)
            sim = jnp.einsum('bhwid,bhwjd->bhwij', bq, bk)
            i = bt[:, :, None]
            j = btk[:, None, :]
            mask = (i < j) | (i > j + WINDOW) | (j == -1)
            sim = jnp.where(mask, -jnp.finfo(sim.dtype).max, sim)
            attn = jax.nn.softmax(sim, axis=-1)
            out = jnp.einsum('bhwij,bhwjd->bhwid', attn, bv)
            return out.reshape(b, h, n, d)

        def _layer(x, wqkv, qs, ksc, wo, lg, lb, w1, b1, w2, b2):
            b, n, _ = x.shape
            h = shift_token(x)
            qkv = h @ wqkv
            q, k, v = jnp.split(qkv, 3, axis=-1)
            to_heads = lambda t: t.reshape(b, n, HEADS, DIM_HEAD).transpose(0, 2, 1, 3)
            q, k, v = (to_heads(q), to_heads(k), to_heads(v))
            q = l2norm(q) * qs
            k = l2norm(k) * ksc
            q, k = rotary_xpos(q, k)
            o = local_attention(q, k, v)
            o = o.transpose(0, 2, 1, 3).reshape(b, n, INNER)
            x = x + o @ wo
            h = shift_token(x)
            mu = h.mean(-1, keepdims=True)
            var = h.var(-1, keepdims=True)
            h = (h - mu) / jnp.sqrt(var + 1e-05) * lg + lb
            h = h @ w1 + b1
            a, g = jnp.split(h, 2, axis=-1)
            h = a * jax.nn.gelu(g, approximate=False)
            x = x + h @ w2 + b2
            return x
        for l in range(DEPTH):
            x = _layer(x, wqkv[l], q_scale[l], k_scale[l], wo[l], ln_g[l], ln_b[l], w1[l], b1[l], w2[l], b2[l])
        return x

    def _L1_attn_ref(x, u_w, u_b, v_w, v_b, o_w, o_b, t_zero, t_pos):
        import jax, jax.numpy as jnp
        import numpy as np
        EMBED = 128
        HEADS = 8
        D1 = 256
        HEAD_DIM = D1 // HEADS
        SEQ = 256
        BATCH = 4
        MAXL = 256
        EPS = 1e-08

        def simple_rms_norm(x, d):
            rms = jnp.linalg.norm(x, axis=-1, keepdims=True) * d ** (-0.5)
            return x / (rms + EPS)

        def toeplitz_causal(v, t_zero, t_pos):
            n = v.shape[2]
            t = jnp.concatenate([t_zero, t_pos[:, :n - 1]], axis=-1)
            m = 2 * n
            vf = jnp.fft.rfft(v, m, axis=2)
            tf = jnp.fft.rfft(t, m, axis=-1)
            y = jnp.fft.irfft(vf * tf[None, :, :, None], m, axis=2)
            return y[:, :, :n]
        shortcut = x
        xn = simple_rms_norm(x, EMBED)
        u = jax.nn.silu(xn @ u_w.T + u_b)
        v = jax.nn.silu(xn @ v_w.T + v_b)
        n, b, _ = v.shape
        vh = v.reshape(n, b, HEADS, HEAD_DIM).transpose(1, 2, 0, 3)
        y = toeplitz_causal(vh, t_zero, t_pos)
        y = y.transpose(2, 0, 1, 3).reshape(n, b, D1)
        out = u * y
        out = out @ o_w.T + o_b + shortcut
        return out

    def _L1_ffn_ref(x, w_router, w1, b1, w2, b2):
        import jax, jax.numpy as jnp
        import numpy as np
        EMBED_DIM = 128
        HIDDEN_DIM = 512
        NUM_EXPERTS = 8
        TOP_K = 2
        orig_shape = x.shape
        xf = x.reshape(-1, EMBED_DIM)
        logits = xf @ w_router
        probs = jax.nn.softmax(logits, axis=-1)
        topk_w, topk_idx = jax.lax.top_k(probs, TOP_K)
        mask = jax.nn.one_hot(topk_idx, NUM_EXPERTS, dtype=xf.dtype)
        weights = jnp.sum(topk_w[..., None] * mask, axis=1)
        h = jnp.einsum('te,ieh->tih', xf, w1) + b1
        h = jax.nn.gelu(h)
        out = jnp.einsum('tih,ihe->tie', h, w2) + b2
        out = jnp.sum(out * weights[..., None], axis=1)
        return out.reshape(orig_shape)
    x = L0_attn_x
    x = x + 0.5 * _L0_ffn_ref(_layernorm(x, axis=-1), L0_ffn_wqkv, L0_ffn_q_scale, L0_ffn_k_scale, L0_ffn_wo, L0_ffn_ln_g, L0_ffn_ln_b, L0_ffn_w1, L0_ffn_b1, L0_ffn_w2, L0_ffn_b2)
    x = x + _L0_attn_ref(_layernorm(x, axis=-1), L0_attn_log_A, L0_attn_B_param, L0_attn_C_param, L0_attn_D_param, L0_attn_log_dt, L0_attn_ln_gamma, L0_attn_ln_beta, L0_attn_W_out, L0_attn_b_out)
    x = x + 0.5 * _L0_ffn_ref(_layernorm(x, axis=-1), L0_ffn_wqkv, L0_ffn_q_scale, L0_ffn_k_scale, L0_ffn_wo, L0_ffn_ln_g, L0_ffn_ln_b, L0_ffn_w1, L0_ffn_b1, L0_ffn_w2, L0_ffn_b2)
    x = x + 0.5 * _L1_ffn_ref(_layernorm(x, axis=-1), L1_ffn_w_router, L1_ffn_w1, L1_ffn_b1, L1_ffn_w2, L1_ffn_b2)
    x = x + _L1_attn_ref(_layernorm(x, axis=-1), L1_attn_u_w, L1_attn_u_b, L1_attn_v_w, L1_attn_v_b, L1_attn_o_w, L1_attn_o_b, L1_attn_t_zero, L1_attn_t_pos)
    x = x + 0.5 * _L1_ffn_ref(_layernorm(x, axis=-1), L1_ffn_w_router, L1_ffn_w1, L1_ffn_b1, L1_ffn_w2, L1_ffn_b2)
    return x

_drawn_inputs = setup_inputs


def setup_inputs(seed=0):
    import zlib

    import numpy as np

    out = dict(_drawn_inputs(seed))
    spreads = {'L0_attn_D_param': (1.0, 0.2),
     'L0_attn_ln_gamma': (1.0, 0.2),
     'L0_attn_ln_beta': (0.0, 0.1),
     'L0_attn_b_out': (0.0, 0.314),
     'L0_ffn_q_scale': (1.0, 0.6),
     'L0_ffn_k_scale': (1.0, 0.6),
     'L0_ffn_ln_g': (1.0, 0.6),
     'L0_ffn_ln_b': (0.0, 0.8),
     'L0_ffn_b1': (0.0, 0.8),
     'L0_ffn_b2': (0.0, 0.1),
     'L1_ffn_b1': (0.0, 2.0),
     'L1_ffn_b2': (0.0, 2.0)}
    factors = {'L0_attn_log_A': 8.0,
     'L0_attn_B_param': 8.0,
     'L0_attn_C_param': 64.0,
     'L0_attn_log_dt': 8.0,
     'L0_ffn_wqkv': 3.898,
     'L0_ffn_wo': 3.882,
     'L0_ffn_w1': 5.72,
     'L0_ffn_w2': 5.601,
     'L1_attn_u_w': 8.0,
     'L1_attn_u_b': 8.0,
     'L1_attn_v_w': 8.0,
     'L1_attn_v_b': 8.0,
     'L1_attn_o_w': 8.0,
     'L1_attn_o_b': 64.0,
     'L1_attn_t_zero': 8.0,
     'L1_ffn_w1': 3.178}
    for name, (base, spread) in spreads.items():
        noise = np.random.default_rng([zlib.crc32(name.encode()), seed]).standard_normal(out[name].shape)
        drawn = base * np.exp(spread * noise) if base else spread * noise
        out[name] = jnp.asarray(drawn.astype(out[name].dtype))
    for name, factor in factors.items():
        out[name] = (out[name] * factor).astype(out[name].dtype)
    return out
```

```python
from contextlib import ExitStack

import numpy as np

import concourse.bass as bass
from concourse import mybir

F32 = mybir.dt.float32
BF16 = mybir.dt.bfloat16
U32 = mybir.dt.uint32
ALU = mybir.AluOpType
ACT = mybir.ActivationFunctionType
AX = mybir.AxisListType

P = 128
T = 2048
DM = 128
C = 512
NCH = T // C
TILES = C // P
HEADS, DH, WIN = 8, 64, 64
HP = HEADS // 2
INNER = HEADS * DH
HID = int(DM * 4 * 2 / 3)
HBLK = [(0, 128), (128, 128), (256, HID - 256)]
NS = 64
L = 64
NL = T // L
NE, MH = 8, 512
MB = MH // P
VW = DH + 1
LN_EPS = 1e-5
CREDIT = 4
LN2 = float(np.log(2.0))
SS_SHIFT = 20
LOG_EXP_SET = 6


def shape_constants():
    f = np.float32
    d = np.arange(0, DH, 2, dtype=f)
    inv_freq = (f(1.0) / np.power(f(10000.0), d / f(DH))).astype(f)
    t = np.arange(T, dtype=f)
    freqs = t[:, None] * inv_freq[None, :]
    base = (d + f(0.4 * DH)) / f(1.4 * DH)
    power = (t - f(T // 2)) / f(WIN // 2)
    scale = np.power(base[None, :], power[:, None]).astype(f)
    two = lambda a: np.concatenate([a, a], 1)
    cos, sin, scale = two(np.cos(freqs)), two(np.sin(freqs)), two(scale)
    sin = sin * np.where(np.arange(DH) < DH // 2, -1.0, 1.0).astype(f)
    qk = [8.0 * cos * scale, 8.0 * sin * scale, cos / scale, sin / scale]
    rot = np.stack([np.concatenate([a.T, a.T], 0) for a in qk], 1).astype(f)

    q, k = np.arange(WIN)[:, None], np.arange(2 * WIN)[None, :]
    own = np.where((k >= q) & (k <= q + WIN), 0.0, -1e30)
    tile = np.concatenate([own, own], 0)
    mask = np.tile(tile, (1, NCH * TILES))
    mask[:WIN, :WIN] = -1e30

    i = np.arange(P)
    ident = np.eye(P)
    centre = ident - 1.0 / DM
    mean = np.full((P, P), 1.0 / DM)
    heads = (i[:, None] // DH == i[None, :] // DH) * 1.0
    flip = ((i[:, None] < L) & (i[:, None] + i[None, :] == L - 1)) * 1.0
    taps = np.tile(L - 1.0 - np.arange(L)[None, :], (P, 1))
    decays = taps + 1.0
    back = -(L - 1.0 - i[:, None] % L)
    expert = np.tile(np.arange(NE)[None, :], (P, 1))
    cols = [ident, centre, mean, heads, flip, taps, decays, expert, back,
            np.full((P, 1), LN_EPS), np.full((P, 1), 2.0 ** (SS_SHIFT - 84)),
            np.full((P, 1), 0.5 * SS_SHIFT * LN2), np.zeros((P, 1))]
    return rot, mask.astype(f), np.concatenate(cols, 1).astype(f)


NPRM_A, NPRM_M = 4, 9
WA_COLS = 3 * INNER + 2 * INNER + HP * DM + NPRM_A
WM_COLS = 2 * HID + 3 * DM + NPRM_M
SSM_COLS = 3 * NS + 5 + 3 * DM + DM + DM
ROUTER_STEPS = 13

SCORES, PROBS, VALUES = 2, 3, 4
PROJECT_V = VALUES - 1
PAIR_OUT = VALUES + 2
OUTPUT = PAIR_OUT + HEADS - 1
DRAIN = OUTPUT - HEADS + 1


def macaron_kernel(nc, ins, out, stages="FSFMUM"):
    with ExitStack() as ctx:
        arena = ctx.enter_context(nc.sbuf_tensor("arena", [P, 53200], F32))
        top = [0]

        def cols(n):
            a = arena[:, top[0]:top[0] + n]
            top[0] += n
            return a

        sems = []

        def sem(name):
            s = ctx.enter_context(nc.semaphore(name))
            sems.append(s)
            return s

        X = cols(T)
        YA, YB = cols(T + 4), cols(T + 4)
        H2 = cols(T)
        ROT = cols(4 * T).rearrange("p (k t) -> p k t", k=4)
        WA, WM = cols(WA_COLS), cols(WM_COLS)
        CST = cols(5 * P + 2 * L + NE + 5)
        MASK = cols(T // 2).bitcast(BF16)
        IDENTB = cols(P // 2).bitcast(BF16)
        R = cols(2 * NE * MH)
        SSMP = cols(SSM_COLS + 2 * DM)
        work = top[0]

        ident, centre, mean, heads_sum, flip = [CST[:, k * P:(k + 1) * P] for k in range(5)]
        o = 5 * P
        taps, decays, expert_id = CST[:, o:o + L], CST[:, o + L:o + 2 * L], CST[:, o + 2 * L:o + 2 * L + NE]
        o += 2 * L + NE
        back, eps_c, tiny_c, unshift_c, zero_c = [CST[:, o + k:o + k + 1] for k in range(5)]

        w_qkv = WA[:, 0:3 * INNER]
        w_rot = WA[:, 3 * INNER:5 * INNER]
        w_o = WA[:, 5 * INNER:5 * INNER + HP * DM].rearrange("p (h n) -> p h n", h=HP)
        prm_a = WA[:, WA_COLS - NPRM_A:WA_COLS]
        w1 = WM[:, 0:2 * HID]
        w2 = WM[:, 2 * HID:2 * HID + 3 * DM].rearrange("p (k n) -> p k n", k=3)
        prm_m = WM[:, WM_COLS - NPRM_M:WM_COLS]

        o = 0
        parts = []
        for n in (NS, NS, NS, 1, 1, 1, 1, 1, DM, DM, DM, DM, DM, DM, DM):
            parts.append(SSMP[:, o:o + n])
            o += n
        (log_a, prm_b, prm_c, log_dt, prm_d, ln_gamma, ln_beta, b_out,
         log_a_t, prm_b_t, prm_c_t, log_dt_row, w_out, edt_row, a64_row) = parts

        HC = cols(C)
        ta, tb = cols(C), cols(C)
        rs, sq, lt, qf, pr, prt = [cols(2 * C).rearrange("p (b n) -> p b n", b=2) for _ in range(6)]
        KP = cols(2 * HP * (C + WIN)).rearrange("p (e h n) -> p e h n", e=2, h=HP)
        V = cols(TILES * HEADS * VW).rearrange("p (t h n) -> p t h n", t=TILES, h=HEADS)
        VS = cols(TILES * HEADS * VW).rearrange("p (t h n) -> p t h n", t=TILES, h=HEADS)
        ON = cols(TILES * INNER).rearrange("p (t n) -> p t n", t=TILES)
        OT = cols(HP * C).rearrange("p (h n) -> p h n", h=HP)
        mx, rec = cols(2 * TILES).rearrange("p (b n) -> p b n", b=2), cols(2 * TILES).rearrange("p (b n) -> p b n", b=2)
        assert top[0] <= 53200, top[0]

        top[0] = work + 9 * C
        GL, HM = [cols(3 * C).rearrange("p (k n) -> p k n", k=3) for _ in range(2)]
        a_c, cb, edt, a_t, cb_t = log_a, prm_b, log_dt, log_a_t, prm_b_t
        KTN = 16
        KT = YA[:, 0:2 * KTN * NS].rearrange("p (b t n) -> p b t n", b=2, t=KTN)
        KC = HC[:, 0:2 * L - 1]
        top[0] = work + C
        A64 = cols(DM * NL).rearrange("p (d c) -> p d c", c=NL)
        top[0] = work + 9 * C
        E = cols(DM * NS)
        UH = cols(DM * NL).rearrange("p (d c) -> p d c", c=NL)
        SS = cols(DM * NL).rearrange("p (d c) -> p d c", c=NL)
        SSO = SS.rearrange("p d c -> p (d c)")[:, 0:T]
        assert top[0] <= 53200
        YS = E[:, 0:DM * NL].rearrange("p (c d) -> p c d", d=DM)
        YT = E[:, DM * NL:DM * NL + T]
        top[0] = work + 9 * C
        HB = cols(2 * MB * C).rearrange("p (b k n) -> p b k n", b=2, k=MB)
        ACC, TMP = cols(C), cols(2 * C).rearrange("p (b n) -> p b n", b=2)
        MB1, MB2, WR = cols(NE * MB), cols(NE * DM), cols(NE)
        PB, WTS, OH, OH2, TOPV = [cols(T // P * NE).rearrange("p (t e) -> p t e", e=NE) for _ in range(5)]
        TOPI = cols(T // P * NE).bitcast(U32).rearrange("p (t e) -> p t e", e=NE)
        IDXF = cols(T // P * NE).rearrange("p (t e) -> p t e", e=NE)
        RM, RSUM = cols(T // P), cols(T // P)
        WU = cols(2 * 256 + 2 * DM + 7)
        UV = cols(4 * C).rearrange("p (k n) -> p k n", k=4)
        assert top[0] <= 53200

        TG = R.rearrange("p (d i) -> p d i", i=L)
        MW1 = R[:, 0:NE * MH].rearrange("p (e n) -> p e n", e=NE)
        MW2 = R[:, NE * MH:2 * NE * MH].rearrange("p (e k n) -> p e k n", e=NE, k=MB)

        bank = [ctx.enter_context(nc.psum_tensor(f"bank{i}", [P, C], F32)) for i in range(8)]
        kernel_dram = nc.dram_tensor("ssm_kernel", [P, 2 * L - 1], F32, kind="Internal")

        x_in, cst_in, rot_in, mask_in, ssm_in, kernel_out, toeplitz_in, e_in = [sem(n) for n in (
            "x_in", "cst_in", "rot_in", "mask_in", "ssm_in", "kernel_out", "toeplitz_in", "e_in")]
        wa_in, wm_in, hc_in, v_carry, v_shift, moe_w_in, moe_s_in, unit_in, x_out = [sem(n) for n in (
            "wa_in", "wm_in", "hc_in", "v_carry", "v_shift", "moe_w_in", "moe_s_in", "unit_in", "x_out")]
        table_dve, table_act, kt_prod, kt_weighed, kt_sum, kt_exp, kt_done, gt_prod, gt_exp, gt_done = [sem(n) for n in (
            "table_dve", "table_act", "kt_prod", "kt_weighed", "kt_sum", "kt_exp", "kt_done", "gt_prod", "gt_exp", "gt_done")]
        mask_done, pool_init, x_ffn, x_ssm, x_unit = [sem(n) for n in (
            "mask_done", "pool_init", "x_ffn", "x_ssm", "x_unit")]
        e_exp, e_prod, e_done, u_mm, u_evac, state_mm, state_evac, state_scan = [sem(n) for n in (
            "e_exp", "e_prod", "e_done", "u_mm", "u_evac", "state_mm", "state_evac", "state_scan")]
        y_mm, y_evac, yt_mm, yt_evac, wout_mm, ssm_sum = [sem(n) for n in (
            "y_mm", "y_evac", "yt_mm", "yt_evac", "wout_mm", "ssm_sum")]
        router_mm, router_dve, router_exp, router_top = [sem(n) for n in (
            "router_mm", "router_dve", "router_exp", "router_top")]
        rms_sq, rms_mm, rms_sqrt, rms_dve, xn_done, uv_mm, uv_silu, gated, uo_mm, unit_sum = [sem(n) for n in (
            "rms_sq", "rms_mm", "rms_sqrt", "rms_dve", "xn_done", "uv_mm", "uv_silu", "gated", "uo_mm", "unit_sum")]
        ln_cen, ln_sq, ln_var, ln_log, ln_rstd, ln_mid, ln_out = [sem("ln_" + n) for n in (
            "cen", "sq", "var", "log", "rstd", "mid", "out")]
        mlp_out, yb_ready = sem("mlp_out"), sem("yb_ready")
        proj, rotated, rot_sum, halo, no_keys, sq_done, ss_mm, ss_log, ss_rstd, unit_done = [sem(n) for n in (
            "proj", "rotated", "rot_sum", "halo", "no_keys", "sq_done", "ss_mm", "ss_log", "ss_rstd", "unit_done")]
        v_mm, v_evac, s_mm, s_max, s_sub, p_exp, pt_mm, pt_evac, o_mm, o_rec, o_norm = [sem(n) for n in (
            "v_mm", "v_evac", "s_mm", "s_max", "s_sub", "p_exp", "pt_mm", "pt_evac", "o_mm", "o_rec", "o_norm")]
        ot_mm, ot_evac, wo_mm = sem("ot_mm"), sem("ot_evac"), sem("wo_mm")
        ag_mm, gl_done, hm_done, w2_mm = sem("ag_mm"), sem("gl_done"), sem("hm_done"), sem("w2_mm")
        h_mm, h_gelu, o2_mm, o2_bias, o2_weighed, o2_acc, acc_mm, x_moe = [sem(n) for n in (
            "h_mm", "h_gelu", "o2_mm", "o2_bias", "o2_weighed", "o2_acc", "acc_mm", "x_moe")]

        def need(eng, s, n):
            eng.wait_ge(s, n + CREDIT)

        def give_credit(eng, mine):
            for s in mine:
                eng.sem_inc(s, CREDIT)

        plan, norms, seen = [], 0, {"F": 0, "S": 0, "M": 0, "U": 0}
        for kind in stages:
            plan.append((kind, norms, seen[kind]))
            norms += {"F": 3, "S": 2, "M": 1, "U": 1}[kind] * NCH
            seen[kind] += 1

        def x_whole(eng, k):
            if k == 0:
                eng.wait_ge(x_in, 16)
                return
            kind, _, run = plan[k - 1]
            if kind == "F":
                eng.wait_ge(x_ffn, run + 1)
            elif kind == "S":
                eng.wait_ge(x_ssm, NCH)
            elif kind == "M":
                need(eng, x_moe, NCH * (run + 1))
            else:
                eng.wait_ge(x_unit, NCH)

        def attention_steps(eng, call, d, step):
            count = 2 * NCH * call

            def run(steps, new, old):
                for t in steps:
                    def at(k):
                        chunk = new if t >= k else old
                        return chunk and ((t - k) % HEADS,) + chunk
                    step(t, at)

            run(range(HEADS), (0, d * NCH + count), None)
            with eng.Fori(0, NCH - 1) as i:
                run(range(HEADS), (i * C + C, d * NCH + i + (count + 1)), (i * C, d * NCH + i + count))
            run(range(DRAIN), None, ((NCH - 1) * C, d * NCH + (count + NCH - 1)))

        block = ctx.enter_context(nc.Block())

        @block.sync
        def _(sp):
            sp.dma_start(CST, ins["cst"]).then_inc(cst_in, 16)
            sp.dma_start(SSMP[:, 0:SSM_COLS], ins["ssm"]).then_inc(ssm_in, 16)
            sp.dma_start(X, ins["x"]).then_inc(x_in, 16)
            sp.dma_start(ON.rearrange("p t n -> p (t n)"), ins["mask"]).then_inc(mask_in, 16)
            sp.dma_start(WA, ins["wa"][0]).then_inc(wa_in, 16)
            sp.dma_start(ROT, ins["rot"]).then_inc(rot_in, 16)
            sp.dma_start(WM, ins["wm"][0]).then_inc(wm_in, 16)

            def load_experts():
                sp.dma_start(MW1, ins["mw1"]).then_inc(moe_w_in, 16)
                sp.dma_start(MW2, ins["mw2"]).then_inc(moe_w_in, 16)

            for k, (kind, norm0, run) in enumerate(plan):
                if kind == "F":
                    call = run
                    sp.wait_ge(pool_init, 3 * (call + 1))
                    need(sp, ln_out, norm0 + NCH)
                    with sp.Fori(0, 2) as d:
                        with sp.Fori(0, NCH) as i:
                            g = d * NCH + i + 2 * NCH * call
                            need(sp, mlp_out, d * NCH + i + (2 * NCH * call - NCH + 1))
                            need(sp, v_mm, g * TILES)
                            sp.dma_start(HC, YA[:, bass.ds(i * C, C)]).then_inc(hc_in, 16)
                            need(sp, o_mm, g * 8)
                            sp.dma_start(VS[0:WIN, 0], V[WIN:P, TILES - 1]).then_inc(v_carry, 16)
                            need(sp, v_evac, g * TILES + TILES)
                            sp.dma_start(VS[WIN:P], V[0:WIN]).then_inc(v_shift, 16)
                            sp.dma_start(VS[0:WIN, 1:TILES], V[WIN:P, 0:TILES - 1]).then_inc(v_shift, 16)
                        need(sp, wo_mm, (d + (2 * call + 1)) * NCH)
                        sp.dma_start(WA, ins["wa"][bass.ds(d + 1, 1)].rearrange("o p n -> (o p) n")).then_inc(wa_in, 16)
                        need(sp, mlp_out, (d + (2 * call + 1)) * NCH)
                        sp.dma_start(WM, ins["wm"][bass.ds(d + 1, 1)].rearrange("o p n -> (o p) n")).then_inc(wm_in, 16)
                if kind == "S":
                    x_whole(sp, k)
                    sp.dma_start(E[0:L], ins["log_a_row"].partition_broadcast(L)).then_inc(e_in, 16)
                    sp.wait_ge(kt_done, 1)
                    sp.dma_start(kernel_dram.ap(), KC).then_inc(kernel_out, 16)
                    sp.wait_ge(kernel_out, 16)
                    sp.dma_start(TG[0:L], bass.AP(kernel_dram.ap().tensor, 0, [[1, L], [2 * L - 1, DM], [1, L]])).then_inc(toeplitz_in, 16)
                    if "M" in stages:
                        sp.wait_ge(x_ssm, NCH)
                        load_experts()
                if kind == "M":
                    if run == 0 and "S" not in stages:
                        load_experts()
                    x_whole(sp, k)
                    sp.dma_start(MB1, ins["mb1"]).then_inc(moe_s_in, 16)
                    sp.dma_start(MB2, ins["mb2"].partition_broadcast(P)).then_inc(moe_s_in, 16)
                    sp.dma_start(WR, ins["mwr"]).then_inc(moe_s_in, 16)
                if kind == "U":
                    x_whole(sp, k)
                    sp.dma_start(WU, ins["unit"]).then_inc(unit_in, 16)
            x_whole(sp, len(plan))
            sp.dma_start(out, X).then_inc(x_out, 16)
            sp.wait_ge(x_out, 16)

        @block.tensor
        def _(pe):
            mm = nc.tensor.matmul
            give_credit(pe, [ln_cen, ln_var, proj, ss_mm, v_mm, s_mm, pt_mm, o_mm, ot_mm, wo_mm,
                             ag_mm, w2_mm, h_mm, o2_mm, acc_mm])

            def norm(src, n0, ready):
                def variance(c):
                    need(pe, ln_sq, n0 + (c + 1))
                    mm(bank[4 + c][:], mean, sq[:, c % 2], start=True, stop=True).then_inc(ln_var, 1)

                for c in range(NCH):
                    ready(c)
                    mm(bank[c][:], centre, src[:, c * C:(c + 1) * C], start=True, stop=True).then_inc(ln_cen, 1)
                    if c:
                        variance(c - 1)
                variance(NCH - 1)

            def attention(call, d):
                def project(u, c, g):
                    if u == 0:
                        need(pe, mlp_out, g + (1 - NCH))
                    need(pe, rotated, g * 8 + u)
                    w0 = (u % 2) * INNER + (u // 2) * P
                    mm(bank[0][:], w_qkv[:, w0:w0 + P], YA[:, bass.ds(c, C)], start=True, stop=True)
                    mm(bank[1][:], w_rot[:, w0:w0 + P], YA[:, bass.ds(c, C)], start=True, stop=True).then_inc(proj, 1)

                def project_v(c, g):
                    pe.wait_ge(hc_in, (g + 1) * 16)
                    for t in range(TILES):
                        if t < 2:
                            need(pe, s_sub, g * 8 + (PROJECT_V - SCORES - 1 + t))
                        else:
                            need(pe, v_evac, g * TILES + (t - 1))
                        mm(bank[3 + (t + PROJECT_V - SCORES) % 2][:], HC[:, t * P:(t + 1) * P], w_qkv[:, 2 * INNER:],
                           start=True, stop=True).then_inc(v_mm, 1)

                def square_sum(u, c, g):
                    need(pe, sq_done, g * 8 + (u + 1))
                    need(pe, ss_log, g * 8 + u)
                    mm(bank[2][:], heads_sum, sq[:, 0], start=True, stop=True).then_inc(ss_mm, 1)

                def scores(h, c, g):
                    hp = h // 2
                    need(pe, unit_done, g * 8 + (2 * hp + 2))
                    need(pe, s_sub, g * 8 + (h - 1))
                    first = PROJECT_V - SCORES
                    if first <= h < first + 2:
                        need(pe, v_evac, g * TILES + (3 + h - first))
                    bk = bank[3 + h % 2]
                    mm(bk[:], IDENTB, MASK[:, bass.ds(c, C)], start=True, stop=False, skip_group_check=True)
                    for w in range(2 * TILES):
                        r0, c0 = WIN * (w % 2), P * (w // 2)
                        last = mm(bk[r0:r0 + WIN, c0:c0 + P], qf[:, hp % 2, w * WIN:(w + 1) * WIN],
                                  KP[:, h % 2, hp, w * WIN:w * WIN + P], start=False, stop=True, skip_group_check=True)
                    last.then_inc(s_mm, 1)

                def transpose_probs(h, c, g):
                    need(pe, p_exp, g * 8 + (h + 1))
                    need(pe, pt_evac, g * 8 + h)
                    for t in range(TILES):
                        last = nc.tensor.transpose(bank[5][:, t * P:(t + 1) * P], pr[:, h % 2, t * P:(t + 1) * P], ident)
                    last.then_inc(pt_mm, 1)

                def values(h, c, g):
                    need(pe, pt_evac, g * 8 + (h + 1))
                    need(pe, o_norm, g * 8 + h)
                    if h == 0:
                        pe.wait_ge(v_shift, (g + 1) * 32)
                    for w in range(2 * TILES):
                        t, r0 = w // 2, WIN * (w % 2)
                        last = mm(bank[6][r0:r0 + WIN, t * VW:(t + 1) * VW], prt[:, h % 2, w * WIN:(w + 1) * WIN],
                                  (VS if w % 2 == 0 else V)[:, t, h, :], start=True, stop=True)
                    last.then_inc(o_mm, 1)

                def transpose_out(hp, g):
                    need(pe, o_norm, g * 8 + (2 * hp + 2))
                    if hp:
                        need(pe, ot_evac, g * HP + hp)
                    else:
                        need(pe, yb_ready, g)
                    for t in range(TILES):
                        last = nc.tensor.transpose(bank[7][:, t * P:(t + 1) * P], ON[:, t, hp * P:(hp + 1) * P], ident)
                    last.then_inc(ot_mm, 1)

                def output(g):
                    need(pe, ot_evac, g * HP + HP)
                    for hp in range(HP):
                        last = mm(bank[7][:], w_o[:, hp], OT[:, hp], start=(hp == 0), stop=(hp == HP - 1))
                    last.then_inc(wo_mm, 1)

                def step(t, at):
                    if at(0):
                        project(*at(0))
                    if at(VALUES):
                        values(*at(VALUES))
                    if t == PROJECT_V and at(0):
                        project_v(*at(0)[1:])
                    if at(0):
                        square_sum(*at(0))
                    if at(PAIR_OUT) and at(PAIR_OUT)[0] % 2 == 0:
                        transpose_out(at(PAIR_OUT)[0] // 2, at(PAIR_OUT)[2])
                    if at(PROBS):
                        transpose_probs(*at(PROBS))
                    if at(SCORES):
                        scores(*at(SCORES))
                    if t == OUTPUT - HEADS and at(HEADS):
                        output(at(HEADS)[2])

                pe.wait_ge(wa_in, (d + (2 * call + 1)) * 16)
                attention_steps(pe, call, d, step)

            def mlp(call, d, n1):
                def hidden(j, c, g):
                    k0, m = HBLK[j]
                    need(pe, hm_done, g * 3 + (j - 2))
                    for half in range(2):
                        last = mm(bank[2 * j + half][0:m, :], w1[:, half * HID + k0:half * HID + k0 + m],
                                  H2[:, bass.ds(c, C)], start=True, stop=True)
                    last.then_inc(ag_mm, 1)

                def output(j, g):
                    need(pe, hm_done, g * 3 + (j + 1))
                    if j == 0:
                        need(pe, mlp_out, g)
                    mm(bank[7][:], w2[0:HBLK[j][1], j], HM[0:HBLK[j][1], j], start=(j == 0), stop=(j == 2)).then_inc(w2_mm, 1)

                g0 = d * NCH + 2 * NCH * call
                pe.wait_ge(wm_in, (d + (2 * call + 1)) * 16)
                need(pe, ln_out, n1 + NCH)
                for j in range(3):
                    hidden(j, 0, g0)
                with pe.Fori(0, NCH - 1) as i:
                    g = d * NCH + i + 2 * NCH * call
                    for j in range(3):
                        hidden(j, i * C + C, g + 1)
                        output(j, g)
                for j in range(3):
                    output(j, g0 + (NCH - 1))

            def ssm(norm0):
                need(pe, ln_out, norm0 + 2 * NCH)
                for q in range(8):
                    if q >= 4:
                        pe.wait_ge(u_evac, q - 3)
                    for k in range(4):
                        c = 4 * q + k
                        last = nc.tensor.transpose(bank[q % 4][0:L, k * P:(k + 1) * P], H2[:, c * L:(c + 1) * L], ident)
                    last.then_inc(u_mm, 1)
                pe.wait_ge(u_evac, 8)
                for q in range(8):
                    if q % 2 == 0:
                        pe.wait_ge(e_done, q // 2 + 1)
                    if q >= 4:
                        pe.wait_ge(state_evac, q - 3)
                    for k in range(16):
                        dd = 16 * q + k
                        last = mm(bank[4 + q % 4][L:P, k * NL:(k + 1) * NL], E[0:L, dd * NS:(dd + 1) * NS], UH[0:L, dd, :], start=True, stop=True)
                    last.then_inc(state_mm, 1)
                pe.wait_ge(toeplitz_in, 16)
                pe.wait_ge(gt_done, 4)
                for q in range(8):
                    if q % 4 == 0:
                        pe.wait_ge(state_scan, q // 4 + 1)
                    if q >= 4:
                        pe.wait_ge(y_evac, q - 3)
                    for k in range(16):
                        dd = 16 * q + k
                        last = mm(bank[q % 4][0:L, k * NL:(k + 1) * NL], TG[:, dd, :], UH[:, dd, :], start=True, stop=True)
                    last.then_inc(y_mm, 1)
                pe.wait_ge(y_evac, 8)
                for q in range(NCH):
                    for k in range(8):
                        last = mm(bank[4 + q][:, k * L:(k + 1) * L], YS[0:L, 8 * q + k, :], flip[0:L, 0:L], start=True, stop=True)
                    last.then_inc(yt_mm, 1)
                for q in range(NCH):
                    pe.wait_ge(yt_evac, q + 1)
                    mm(bank[q][:], w_out, YT[:, q * C:(q + 1) * C], start=True, stop=True).then_inc(wout_mm, 1)

            def mixture(norm0, moe):
                pe.wait_ge(moe_w_in, 32)
                pe.wait_ge(moe_s_in, 48 * (moe + 1))
                need(pe, ln_out, norm0 + NCH)
                for t in range(T // P):
                    last = mm(bank[7][:, t * NE:(t + 1) * NE], YB[:, t * P:(t + 1) * P], WR, start=True, stop=True)
                last.then_inc(router_mm, 1)

                def hidden(e, c, g):
                    for j in range(MB):
                        need(pe, h_gelu, g * (NE * MB) + (e * MB + j - MB + 1))
                        mm(bank[j][:], MW1[:, e, j * P:(j + 1) * P], YB[:, bass.ds(c, C)], start=True, stop=True).then_inc(h_mm, 1)

                def expert_out(e, g):
                    need(pe, h_gelu, g * (NE * MB) + (e + 1) * MB)
                    need(pe, o2_bias, g * NE + (e - 1))
                    for t in range(TILES):
                        for j in range(MB):
                            last = mm(bank[4 + e % 2][:, t * P:(t + 1) * P], HB[:, e % 2, j, t * P:(t + 1) * P], MW2[:, e, j],
                                      start=(j == 0), stop=(j == MB - 1))
                    last.then_inc(o2_mm, 1)

                def transpose_sum(g):
                    need(pe, o2_acc, g * NE + NE)
                    need(pe, x_moe, g)
                    for t in range(TILES):
                        last = nc.tensor.transpose(bank[6][:, t * P:(t + 1) * P], ACC[:, t * P:(t + 1) * P], ident)
                    last.then_inc(acc_mm, 1)

                def chunk(c, g, before):
                    for e in range(NE):
                        hidden(e, c, g)
                        if e > 0:
                            if e == 1 and before is not None:
                                transpose_sum(before)
                            expert_out(e - 1, g)
                        elif before is not None:
                            expert_out(NE - 1, before)

                chunk(0, NCH * moe, None)
                with pe.Fori(0, NCH - 1) as i:
                    chunk(i * C + C, i + (NCH * moe + 1), i + NCH * moe)
                expert_out(NE - 1, NCH * moe + NCH - 1)
                transpose_sum(NCH * moe + NCH - 1)

            def unit(norm0):
                pe.wait_ge(unit_in, 16)
                for c in range(NCH):
                    pe.wait_ge(rms_sq, c + 1)
                    if c >= 2:
                        pe.wait_ge(rms_sqrt, c - 1)
                    mm(bank[6 + c % 2][:], mean, sq[:, c % 2], start=True, stop=True).then_inc(rms_mm, 1)
                for c in range(NCH):
                    pe.wait_ge(xn_done, c + 1)
                    for k in range(4):
                        if c:
                            pe.wait_ge(uv_silu, 4 * (c - 1) + k + 1)
                        mm(bank[k][:], WU[:, k * P:(k + 1) * P], H2[:, c * C:(c + 1) * C], start=True, stop=True).then_inc(uv_mm, 1)
                    pe.wait_ge(gated, 2 * c + 2)
                    if c >= 2:
                        pe.wait_ge(unit_sum, c - 1)
                    for k in range(2):
                        last = mm(bank[4 + c % 2][:], WU[:, 4 * P + k * P:4 * P + (k + 1) * P], UV[:, k], start=(k == 0), stop=(k == 1))
                    last.then_inc(uo_mm, 1)

            pe.wait_ge(cst_in, 16)
            pe.wait_ge(mask_done, 1)
            for k, (kind, norm0, run) in enumerate(plan):
                x_whole(pe, k)
                norm(X, norm0, lambda c: None)
                if kind == "F":
                    need(pe, ln_out, norm0 + NCH)
                    with pe.Fori(0, 2) as d:
                        attention(run, d)
                        n1 = d * NCH + (norm0 + NCH)
                        norm(YB, n1, lambda c: need(pe, yb_ready, d * NCH + c + (2 * NCH * run + 1)))
                        mlp(run, d, n1)
                elif kind == "S":
                    norm(YB, norm0 + NCH, lambda c: need(pe, ln_out, c + (norm0 + 1)))
                    ssm(norm0)
                elif kind == "M":
                    mixture(norm0, run)
                elif kind == "U":
                    unit(norm0)

        @block.scalar
        def _(act):
            A = nc.scalar.activation
            give_credit(act, [ln_sq, ln_log, ln_rstd, sq_done, ss_log, ss_rstd, v_evac, p_exp, pt_evac,
                              ot_evac, gl_done, h_gelu])

            def log_exp_table():
                act.add_instruction(mybir.InstLoadActFuncSet(
                    act_func_set_id=LOG_EXP_SET, name=nc.get_next_instruction_name(),
                    engine=mybir.EngineType.Activation))

            def norm(n0):
                for c in range(NCH + 1):
                    if c < NCH:
                        need(act, ln_cen, n0 + (c + 1))
                        need(act, ln_var, n0 + (c - 1))
                        A(sq[:, c % 2], bank[c][:], ACT.Square).then_inc(ln_sq, 1)
                    if c:
                        need(act, ln_var, n0 + c)
                        need(act, ln_rstd, n0 + (c - 2))
                        A(lt[:, (c - 1) % 2], bank[3 + c][:], ACT.Ln, bias=eps_c).then_inc(ln_log, 1)
                        need(act, ln_log, n0 + c)
                        need(act, ln_out, n0 + (c - 2))
                        A(rs[:, (c - 1) % 2], lt[:, (c - 1) % 2], ACT.Exp, scale=-0.5, bias=zero_c).then_inc(ln_rstd, 1)

            def attention(call, d):
                def square(u, c, g):
                    need(act, proj, g * 8 + (u + 1))
                    A(sq[:, 0], bank[0][:], ACT.Square).then_inc(sq_done, 1)

                def evacuate_v(c, g):
                    for t in range(TILES):
                        need(act, v_mm, g * TILES + (t + 1))
                        if t == TILES - 1:
                            act.wait_ge(v_carry, (g + 1) * 16)
                        A(V[:, t, :, 0:DH], bank[3 + (t + PROJECT_V - SCORES) % 2][:].rearrange("p (h n) -> p h n", h=HEADS),
                          ACT.Copy).then_inc(v_evac, 1)

                def inverse_norm(u, c, g):
                    need(act, ss_mm, g * 8 + (u + 1))
                    A(lt[:, 0], bank[2][:], ACT.Ln, scale=2.0 ** SS_SHIFT, bias=tiny_c).then_inc(ss_log, 1)
                    need(act, ss_log, g * 8 + (u + 1))
                    A(rs[:, u % 2], lt[:, 0], ACT.Exp, scale=-0.5, bias=unshift_c).then_inc(ss_rstd, 1)

                def exp(h, c, g):
                    need(act, s_sub, g * 8 + (h + 1))
                    A(pr[:, h % 2], pr[:, h % 2], ACT.Exp, bias=zero_c).then_inc(p_exp, 1)

                def evacuate_probs(h, c, g):
                    need(act, pt_mm, g * 8 + (h + 1))
                    A(prt[:, h % 2], bank[5][:], ACT.Copy).then_inc(pt_evac, 1)

                def evacuate_out(hp, g):
                    need(act, ot_mm, g * HP + (hp + 1))
                    A(OT[:, hp], bank[7][:], ACT.Copy).then_inc(ot_evac, 1)

                def step(t, at):
                    if at(0):
                        square(*at(0))
                    if at(PROBS):
                        exp(*at(PROBS))
                    if t == PROJECT_V and at(0):
                        evacuate_v(*at(0)[1:])
                    if at(0):
                        inverse_norm(*at(0))
                    if at(PAIR_OUT) and at(PAIR_OUT)[0] % 2 == 0:
                        evacuate_out(at(PAIR_OUT)[0] // 2, at(PAIR_OUT)[2])
                    if at(PROBS):
                        evacuate_probs(*at(PROBS))

                attention_steps(act, call, d, step)

            def mlp(call, d):
                with act.Fori(0, NCH) as i:
                    g = d * NCH + i + 2 * NCH * call
                    for j, (k0, m) in enumerate(HBLK):
                        need(act, ag_mm, g * 3 + (j + 1))
                        A(GL[0:m, j], bank[2 * j + 1][0:m, :], ACT.Gelu, bias=prm_m[0:m, 5 + j:6 + j]).then_inc(gl_done, 1)

            def small_tables():
                act.wait_ge(ssm_in, 16)
                A(a_c, log_a, ACT.Exp, bias=zero_c).then_inc(table_act, 1)
                A(edt, log_dt, ACT.Exp, bias=zero_c).then_inc(table_act, 1)
                A(a_t[L:P], log_a_t[L:P], ACT.Exp, bias=zero_c[L:P]).then_inc(table_act, 1)
                A(edt_row, log_dt_row, ACT.Exp, bias=zero_c).then_inc(table_act, 1)

            def tables():
                for b in range(L // KTN):
                    act.wait_ge(kt_prod, b + 1)
                    A(KT[:, b % 2], KT[:, b % 2], ACT.Exp, bias=zero_c).then_inc(kt_exp, 1)
                for q in range(4):
                    act.wait_ge(gt_prod, q + 1)
                    v = TG[L:P, 32 * q:32 * q + 32, :]
                    A(v, v, ACT.Exp, bias=zero_c[L:P]).then_inc(gt_exp, 1)

            def ssm(norm0):
                A(a64_row[L:P], a_t[L:P], ACT.Exp, scale=float(L), bias=zero_c[L:P]).then_inc(table_act, 1)
                act.wait_ge(e_in, 16)
                q4 = DM * NS // 4
                for q in range(4):
                    v = E[0:L, q * q4:(q + 1) * q4]
                    A(v, v, ACT.Exp, bias=zero_c[0:L]).then_inc(e_exp, 1)
                for q in range(4):
                    v = E[0:L, q * q4:(q + 1) * q4]
                    act.wait_ge(e_prod, q + 1)
                    A(v, v, ACT.Exp, scale=back[0:L], bias=zero_c[0:L]).then_inc(e_done, 1)
                for q in range(8):
                    act.wait_ge(u_mm, q + 1)
                    A(UH[0:L, :, 4 * q:4 * q + 4], bank[q % 4][0:L, :].rearrange("p (c d) -> p d c", d=DM),
                      ACT.Copy).then_inc(u_evac, 1)
                tables()
                act.wait_ge(state_mm, 8)
                for q in range(8):
                    act.wait_ge(y_mm, q + 1)
                    A(YS[0:L, :, 16 * q:16 * q + 16], bank[q % 4][0:L, :].rearrange("p (d c) -> p c d", c=NL),
                      ACT.Copy).then_inc(y_evac, 1)
                for q in range(NCH):
                    act.wait_ge(yt_mm, q + 1)
                    A(YT[:, q * C:(q + 1) * C], bank[4 + q][:], ACT.Copy).then_inc(yt_evac, 1)

            def mixture(moe):
                act.wait_ge(moe_s_in, 48 * (moe + 1))
                act.wait_ge(router_dve, ROUTER_STEPS * moe + 2)
                A(PB, PB, ACT.Exp, bias=zero_c).then_inc(router_exp, 1)
                with act.Fori(0, NCH) as i:
                    g = i + NCH * moe
                    for e in range(NE):
                        need(act, o2_mm, g * NE + (e - 1))
                        for j in range(MB):
                            need(act, h_mm, g * (NE * MB) + (e * MB + j + 1))
                            A(HB[:, e % 2, j], bank[j][:], ACT.Gelu_apprx_tanh,
                              bias=MB1[:, e * MB + j:e * MB + j + 1]).then_inc(h_gelu, 1)

            def unit(norm0):
                act.wait_ge(unit_in, 16)
                need(act, ln_out, norm0 + NCH)
                for c in range(NCH):
                    if c >= 2:
                        act.wait_ge(rms_mm, c - 1)
                    A(sq[:, c % 2], YB[:, c * C:(c + 1) * C], ACT.Square).then_inc(rms_sq, 1)
                for c in range(NCH):
                    act.wait_ge(rms_mm, c + 1)
                    A(H2[:, c * C:(c + 1) * C], bank[6 + c % 2][:], ACT.Sqrt, bias=zero_c).then_inc(rms_sqrt, 1)
                for c in range(NCH):
                    if c:
                        act.wait_ge(uo_mm, c)
                    for k in range(4):
                        act.wait_ge(uv_mm, 4 * c + k + 1)
                        A(UV[:, k], bank[k][:], ACT.Silu, bias=WU[:, 6 * P + k:6 * P + k + 1]).then_inc(uv_silu, 1)

            act.wait_ge(cst_in, 16)
            log_exp_table()
            small_tables()
            for k, (kind, norm0, run) in enumerate(plan):
                norm(norm0)
                if kind == "F":
                    with act.Fori(0, 2) as d:
                        attention(run, d)
                        norm(d * NCH + (norm0 + NCH))
                        mlp(run, d)
                        log_exp_table()
                elif kind == "S":
                    norm(norm0 + NCH)
                    ssm(norm0)
                elif kind == "M":
                    mixture(run)
                    log_exp_table()
                elif kind == "U":
                    unit(norm0)
                    log_exp_table()

        @block.vector
        def _(dve):
            TT = nc.vector.tensor_tensor
            STT = nc.vector.scalar_tensor_tensor
            give_credit(dve, [ln_mid, ln_out, mlp_out, yb_ready, rotated, unit_done, s_max, s_sub, o_rec, o_norm,
                              hm_done, o2_bias, o2_weighed, o2_acc, x_moe])
            halves = ((0, DH, 0), (DH, P, 1))

            def wide(v, n):
                return v.unsqueeze(2).to_broadcast([v.shape[0], v.shape[1], n])

            def across(v, n):
                return v.unsqueeze(1).to_broadcast([v.shape[0], n, v.shape[1]])

            def small_tables():
                dve.wait_ge(ssm_in, 16)
                TT(cb, prm_c, prm_b, ALU.mult).then_inc(table_dve, 1)
                TT(cb_t[L:P], prm_c_t[L:P], prm_b_t[L:P], ALU.mult).then_inc(table_dve, 1)
                dve.wait_ge(table_dve, 2)
                dve.wait_ge(table_act, 4)
                nc.vector.tensor_scalar(a_c, a_c, edt, -1.0, ALU.mult, ALU.mult).then_inc(table_dve, 1)
                nc.vector.tensor_scalar(cb, cb, edt, None, ALU.mult).then_inc(table_dve, 1)
                STT(out=a_t[L:P], in0=a_t[L:P], scalar=-1.0, in1=edt_row[L:P], op0=ALU.mult, op1=ALU.mult).then_inc(table_dve, 1)
                TT(cb_t[L:P], cb_t[L:P], edt_row[L:P], ALU.mult).then_inc(table_dve, 1)

            def tables():
                nc.vector.memset(KC[:, L:2 * L - 1], 0.0)
                taps_at = lambda b: slice(KTN * b, KTN * b + KTN)

                for b in range(L // KTN + 1):
                    if b < L // KTN:
                        if b >= 2:
                            dve.wait_ge(kt_sum, b - 1)
                        TT(KT[:, b % 2], wide(taps[:, taps_at(b)], NS), across(a_c, KTN), ALU.mult).then_inc(kt_prod, 1)
                    if b:
                        v = KT[:, (b - 1) % 2]
                        dve.wait_ge(kt_exp, b)
                        TT(v, v, across(cb, KTN), ALU.mult).then_inc(kt_weighed, 1)
                        dve.wait_ge(kt_weighed, b)
                        nc.vector.tensor_reduce(KC[:, taps_at(b - 1)], v, AX.X, ALU.add).then_inc(kt_sum, 1)
                dve.wait_ge(kt_sum, L // KTN)
                TT(KC[:, L - 1:L], KC[:, L - 1:L], prm_d, ALU.add).then_inc(kt_done, 1)
                for q in range(5):
                    if q < 4:
                        TT(TG[L:P, 32 * q:32 * q + 32, :], wide(a_t[L:P, 32 * q:32 * q + 32], L), across(decays[L:P], 32),
                           ALU.mult).then_inc(gt_prod, 1)
                    if q:
                        dve.wait_ge(gt_exp, q)
                        v = TG[L:P, 32 * q - 32:32 * q, :]
                        TT(v, v, wide(cb_t[L:P, 32 * q - 32:32 * q], L), ALU.mult).then_inc(gt_done, 1)

            def norm_chunks(n0, write):
                for c in range(NCH):
                    need(dve, ln_rstd, n0 + (c + 1))
                    write(c, n0 + c)

            def plain(c, n):
                TT(YB[:, c * C:(c + 1) * C], bank[c][:], rs[:, c % 2], ALU.mult).then_inc(ln_out, 1)

            def shifted(c, n):
                for p0, p1, shift in halves:
                    last = TT(YA[p0:p1, c * C + shift:(c + 1) * C + shift], bank[c][p0:p1, :], rs[p0:p1, c % 2], ALU.mult)
                last.then_inc(ln_out, 1)

            def affine(gain, bias):
                def write(c, n):
                    buf = (ta, tb)[c % 2]
                    if c >= 2:
                        need(dve, ln_out, n - 1)
                    TT(buf, bank[c][:], rs[:, c % 2], ALU.mult).then_inc(ln_mid, 1)
                    need(dve, ln_mid, n_mid[0] + n)
                    nc.vector.tensor_scalar(H2[:, c * C:(c + 1) * C], buf, gain, bias, ALU.mult, ALU.add).then_inc(ln_out, 1)
                return write

            def attention(call, d):
                def rotate(u, c, g):
                    k = u % 2
                    chunk = bass.ds(c, C)
                    need(dve, proj, g * 8 + (u + 1))
                    STT(out=tb, in0=bank[1][:], scalar=prm_a[:, 2 * k + 1:2 * k + 2], in1=ROT[:, 2 * k + 1, chunk],
                        op0=ALU.mult, op1=ALU.mult)
                    need(dve, sq_done, g * 8 + (u + 1))
                    need(dve, unit_done, g * 8 + u)
                    STT(out=ta, in0=bank[0][:], scalar=prm_a[:, 2 * k:2 * k + 1], in1=ROT[:, 2 * k, chunk],
                        op0=ALU.mult, op1=ALU.mult).then_inc(rotated, 1)

                def normalise(u, c, g):
                    hp = u // 2
                    need(dve, ss_rstd, g * 8 + (u + 1))
                    need(dve, rot_sum, g * 8 + (u + 1))
                    if u % 2 == 0:
                        last = STT(out=qf[:, hp % 2], in0=rs[:, 0], scalar=1e12, in1=ta, op0=ALU.min, op1=ALU.mult)
                    else:
                        need(dve, halo, g * HP + (hp + 1))
                        for e in range(2):
                            p0, p1 = e * DH, (e + 1) * DH
                            last = STT(out=KP[p0:p1, e, hp, WIN:WIN + C], in0=rs[p0:p1, 1], scalar=1e12,
                                       in1=ta[p0:p1], op0=ALU.min, op1=ALU.mult)
                    last.then_inc(unit_done, 1)

                def softmax(h, c, g):
                    by_row = lambda a: a.rearrange("p (t k) -> p t k", t=TILES)
                    need(dve, s_mm, g * 8 + (h + 1))
                    nc.vector.tensor_reduce(mx[:, h % 2], by_row(bank[3 + h % 2][:]), AX.X, ALU.max).then_inc(s_max, 1)
                    need(dve, s_max, g * 8 + (h + 1))
                    TT(by_row(pr[:, h % 2]), by_row(bank[3 + h % 2][:]), wide(mx[:, h % 2], P), ALU.subtract).then_inc(s_sub, 1)

                def divide(h, c, g):
                    o = bank[6][:, 0:TILES * VW].rearrange("p (t n) -> p t n", n=VW)
                    need(dve, o_mm, g * 8 + (h + 1))
                    nc.vector.reciprocal(rec[:, h % 2].unsqueeze(2), o[:, :, DH:VW]).then_inc(o_rec, 1)
                    need(dve, o_rec, g * 8 + (h + 1))
                    TT(ON[:, :, h * DH:(h + 1) * DH], o[:, :, 0:DH], wide(rec[:, h % 2], DH), ALU.mult).then_inc(o_norm, 1)

                def residual(c, g):
                    need(dve, wo_mm, g + 1)
                    for p0, p1, shift in halves:
                        to = bass.ds(c + shift, C)
                        last = TT(YB[p0:p1, to], bank[7][p0:p1, :], YA[p0:p1, to], ALU.add)
                    last.then_inc(yb_ready, 1)

                def step(t, at):
                    if at(0):
                        rotate(*at(0))
                    if at(VALUES):
                        divide(*at(VALUES))
                    if at(0):
                        normalise(*at(0))
                    if at(SCORES):
                        softmax(*at(SCORES))
                    if t == OUTPUT - HEADS and at(HEADS):
                        residual(*at(HEADS)[1:])

                dve.wait_ge(wa_in, (d + (2 * call + 1)) * 16)
                attention_steps(dve, call, d, step)

            def mlp(call, d):
                def gate(c, g):
                    for j, (k0, m) in enumerate(HBLK):
                        need(dve, gl_done, g * 3 + (j + 1))
                        need(dve, w2_mm, g * 3 + (j - 2))
                        STT(out=HM[0:m, j], in0=bank[2 * j][0:m, :], scalar=prm_m[0:m, 2 + j:3 + j], in1=GL[0:m, j],
                            op0=ALU.add, op1=ALU.mult).then_inc(hm_done, 1)

                def residual(c, g):
                    need(dve, w2_mm, g * 3 + 3)
                    for p0, p1, shift in halves:
                        to = bass.ds(c + shift, C)
                        last = STT(out=YA[p0:p1, to], in0=bank[7][p0:p1, :], scalar=prm_m[p0:p1, 8:9], in1=YB[p0:p1, to],
                                   op0=ALU.add, op1=ALU.add)
                    last.then_inc(mlp_out, 1)

                g0 = d * NCH + 2 * NCH * call
                gate(0, g0)
                with dve.Fori(0, NCH - 1) as i:
                    g = d * NCH + i + 2 * NCH * call
                    gate(i * C + C, g + 1)
                    residual(i * C, g)
                residual((NCH - 1) * C, g0 + (NCH - 1))

            def ssm(norm0):
                need(dve, ln_out, norm0 + 2 * NCH)
                dve.wait_ge(table_act, 5)
                nc.vector.tensor_copy(A64[L:P], wide(a64_row[L:P], NL)).then_inc(ssm_sum, 1)
                dve.wait_ge(ssm_sum, 1)
                nc.vector.memset(A64[L:P, :, 0:1], 0.0).then_inc(ssm_sum, 1)
                nc.vector.memset(SS[L:P, :, 0:1], 0.0).then_inc(ssm_sum, 1)
                for q in range(4):
                    dve.wait_ge(e_exp, q + 1)
                    v = E[0:L, q * (DM * NS // 4):(q + 1) * (DM * NS // 4)].rearrange("p (d n) -> p d n", n=NS)
                    TT(v, v, wide(edt_row[0:L, 32 * q:32 * q + 32], NS), ALU.mult).then_inc(e_prod, 1)
                tables()
                for q in range(8):
                    dve.wait_ge(state_mm, q + 1)
                    nc.vector.tensor_copy(SS[L:P, 16 * q:16 * q + 16, 1:NL],
                                          bank[4 + q % 4][L:P, :].rearrange("p (d c) -> p d c", c=NL)[:, :, 0:NL - 1]).then_inc(state_evac, 1)
                    if q % 4 == 3:
                        dve.wait_ge(state_evac, q + 1)
                        dve.wait_ge(ssm_sum, 3)
                        flat = lambda a: a[L:P, 64 * (q // 4):64 * (q // 4) + 64, :].rearrange("p d c -> p (d c)")
                        nc.vector.tensor_tensor_scan(flat(UH), flat(A64), flat(SS), 0.0, ALU.mult, ALU.add).then_inc(state_scan, 1)
                for q in range(NCH):
                    c = slice(q * C, (q + 1) * C)
                    dve.wait_ge(wout_mm, q + 1)
                    STT(out=SSO[:, c], in0=bank[q][:], scalar=b_out, in1=YB[:, c], op0=ALU.add, op1=ALU.add).then_inc(ssm_sum, 1)
                    dve.wait_ge(ssm_sum, 4 + q)
                    TT(X[:, c], X[:, c], SSO[:, c], ALU.add).then_inc(x_ssm, 1)

            def mixture(moe):
                n = [ROUTER_STEPS * moe]

                def chained(instruction):
                    instruction.then_inc(router_dve, 1)
                    n[0] += 1
                    dve.wait_ge(router_dve, n[0])

                rt = bank[7][:, 0:T // P * NE].rearrange("p (t e) -> p t e", e=NE)
                dve.wait_ge(router_mm, moe + 1)
                chained(nc.vector.tensor_reduce(RM, rt, AX.X, ALU.max))
                chained(TT(PB, rt, wide(RM, NE), ALU.subtract))
                dve.wait_ge(router_exp, moe + 1)
                chained(nc.vector.tensor_reduce(RSUM, PB, AX.X, ALU.add))
                chained(nc.vector.reciprocal(RSUM, RSUM))
                chained(TT(PB, PB, wide(RSUM, NE), ALU.mult))
                for t in range(T // P):
                    last = nc.vector.max(TOPV[:, t], PB[:, t])
                chained(last)
                for t in range(T // P):
                    last = nc.vector.max_index(TOPI[:, t], TOPV[:, t], PB[:, t])
                chained(last)
                chained(nc.vector.tensor_copy(IDXF, TOPI))
                for k, oh in enumerate((WTS, OH)):
                    chained(TT(oh, across(expert_id, T // P), IDXF[:, :, k:k + 1].to_broadcast([P, T // P, NE]), ALU.is_equal))
                    chained(TT(oh, oh, TOPV[:, :, k:k + 1].to_broadcast([P, T // P, NE]), ALU.mult))
                chained(TT(WTS, WTS, OH, ALU.add))
                assert n[0] == ROUTER_STEPS * (moe + 1)
                with dve.Fori(0, NCH) as i:
                    g = i + NCH * moe
                    tiles = lambda a: a.rearrange("p (t n) -> p t n", t=TILES)
                    for e in range(NE):
                        tmp = TMP[:, e % 2]
                        need(dve, o2_mm, g * NE + (e + 1))
                        TT(tiles(tmp), tiles(bank[4 + e % 2][:]), across(MB2[:, e * DM:(e + 1) * DM], TILES), ALU.add).then_inc(o2_bias, 1)
                        need(dve, o2_bias, g * NE + (e + 1))
                        w = WTS[:, bass.ds(i * TILES, TILES), e:e + 1].to_broadcast([P, TILES, DM])
                        if e == 0:
                            need(dve, acc_mm, g)
                        TT(tiles(tmp if e else ACC), tiles(tmp), w, ALU.mult).then_inc(o2_weighed if e else o2_acc, 1)
                        if e:
                            need(dve, o2_weighed, g * (NE - 1) + e)
                            TT(ACC, ACC, tmp, ALU.add).then_inc(o2_acc, 1)
                        need(dve, o2_acc, g * NE + (e + 1))
                    need(dve, acc_mm, g + 1)
                    c = bass.ds(i * C, C)
                    STT(out=X[:, c], in0=bank[6][:], scalar=0.5, in1=X[:, c], op0=ALU.mult, op1=ALU.add).then_inc(x_moe, 1)

            def unit():
                for c in range(NCH):
                    r = H2[:, c * C:(c + 1) * C]
                    dve.wait_ge(rms_sqrt, c + 1)
                    nc.vector.tensor_scalar(r, r, 1e-8, None, ALU.add).then_inc(rms_dve, 1)
                    dve.wait_ge(rms_dve, 2 * c + 1)
                    nc.vector.reciprocal(r, r).then_inc(rms_dve, 1)
                    dve.wait_ge(rms_dve, 2 * c + 2)
                    TT(r, YB[:, c * C:(c + 1) * C], r, ALU.mult).then_inc(xn_done, 1)
                for c in range(NCH):
                    cc = slice(c * C, (c + 1) * C)
                    dve.wait_ge(uv_silu, 4 * c + 4)
                    for k in range(2):
                        STT(out=UV[:, k], in0=UV[:, k], scalar=WU[:, 6 * P + 4 + k:6 * P + 5 + k], in1=UV[:, 2 + k],
                            op0=ALU.mult, op1=ALU.mult).then_inc(gated, 1)
                    dve.wait_ge(uo_mm, c + 1)
                    STT(out=lt[:, c % 2], in0=bank[4 + c % 2][:], scalar=WU[:, 6 * P + 6:6 * P + 7], in1=YB[:, cc],
                        op0=ALU.add, op1=ALU.add).then_inc(unit_sum, 1)
                    dve.wait_ge(unit_sum, c + 1)
                    TT(X[:, cc], X[:, cc], lt[:, c % 2], ALU.add).then_inc(x_unit, 1)

            dve.wait_ge(cst_in, 16)
            dve.wait_ge(mask_in, 16)
            nc.vector.tensor_copy(MASK, ON.rearrange("p t n -> p (t n)"))
            nc.vector.tensor_copy(IDENTB, ident).then_inc(mask_done, 1)
            small_tables()
            dve.wait_ge(rot_in, 16)
            affines = 0
            for k, (kind, norm0, run) in enumerate(plan):
                if kind == "F":
                    nc.vector.memset(YA[DH:P, 0:1], 0.0)
                norm_chunks(norm0, shifted if kind == "F" else plain)
                if kind == "F":
                    n_mid = [affines + 1 - (norm0 + NCH)]
                    nc.vector.memset(YB[DH:P, 0:1], 0.0)
                    with dve.Fori(0, 2) as d:
                        attention(run, d)
                        dve.wait_ge(wm_in, (d + (2 * run + 1)) * 16)
                        norm_chunks(d * NCH + (norm0 + NCH), affine(prm_m[:, 0:1], prm_m[:, 1:2]))
                        mlp(run, d)
                    affines += 2 * NCH
                    need(dve, mlp_out, 2 * NCH * (run + 1))
                    for p0, p1, shift in halves:
                        last = STT(out=X[p0:p1, :], in0=YA[p0:p1, shift:shift + T], scalar=0.5, in1=X[p0:p1, :],
                                   op0=ALU.mult, op1=ALU.add)
                    last.then_inc(x_ffn, 1)
                elif kind == "S":
                    n_mid = [affines + 1 - (norm0 + NCH)]
                    norm_chunks(norm0 + NCH, affine(ln_gamma, ln_beta))
                    affines += NCH
                    ssm(norm0)
                elif kind == "M":
                    mixture(run)
                elif kind == "U":
                    unit()

        @block.gpsimd
        def _(pool):
            give_credit(pool, [rot_sum, halo])
            pool.wait_ge(cst_in, 16)
            for k, (kind, norm0, run) in enumerate(plan):
                if kind != "F":
                    continue
                if k:
                    x_whole(pool, k)
                nc.gpsimd.memset(KP, 0.0).then_inc(pool_init, 1)
                nc.gpsimd.memset(V, 0.0).then_inc(pool_init, 1)
                pool.wait_ge(pool_init, 3 * run + 2)
                nc.gpsimd.memset(V[:, :, :, DH:VW], 1.0).then_inc(pool_init, 1)
                with pool.Fori(0, 2) as d:
                    need(pool, s_mm, (d + 2 * run) * (NCH * 8))
                    zeros = zero_c.unsqueeze(2).to_broadcast([P, HP, WIN])
                    for e in range(2):
                        last = nc.gpsimd.tensor_tensor(KP[:, e, :, C:C + WIN], zeros, zeros, ALU.add)
                    last.then_inc(no_keys, 1)
                    with pool.Fori(0, NCH) as i:
                        g = d * NCH + i + 2 * NCH * run
                        pool.wait_ge(no_keys, d + (2 * run + 1))
                        for u in range(2 * HP):
                            need(pool, rotated, g * 8 + (u + 1))
                            nc.gpsimd.tensor_tensor(ta, ta, tb, ALU.add).then_inc(rot_sum, 1)
                            if u % 2:
                                nc.gpsimd.tensor_copy(KP[:, :, u // 2, 0:WIN], KP[:, :, u // 2, C:C + WIN]).then_inc(halo, 1)


def kernel(**inputs):
    from concourse.bacc import Bacc
    from concourse.bass_utils import run_bass_kernel_spmd

    a = {k: np.asarray(v) for k, v in inputs.items()}
    rot, mask, cst = shape_constants()
    col = lambda v: v.reshape(-1, 1)
    half = DH // 2

    def swapped(w):
        return w.reshape(DM, -1, 2, half)[:, :, ::-1, :].reshape(DM, -1)

    wa, wm = [], []
    for l in range(2):
        wqkv, qs, ks = a["L0_ffn_wqkv"][l], a["L0_ffn_q_scale"][l], a["L0_ffn_k_scale"][l]
        turn = lambda s: np.concatenate([s[half:], s[:half]])
        twice = lambda s: col(np.concatenate([s, s]))
        wo = a["L0_ffn_wo"][l].reshape(HP, P, DM).transpose(1, 0, 2).reshape(P, HP * DM)
        wa.append(np.concatenate([wqkv, swapped(wqkv[:, :2 * INNER]), wo,
                                  twice(qs), twice(turn(qs)), twice(ks), twice(turn(ks))], 1))
        w2 = np.zeros((3 * P, DM), np.float32)
        w2[:HID] = a["L0_ffn_w2"][l]
        b1 = np.zeros((2, 3 * P), np.float32)
        b1[:, :HID] = a["L0_ffn_b1"][l].reshape(2, HID)
        wm.append(np.concatenate([a["L0_ffn_w1"][l], w2.reshape(3, P, DM).transpose(1, 0, 2).reshape(P, 3 * DM),
                                  col(a["L0_ffn_ln_g"][l]), col(a["L0_ffn_ln_b"][l]), b1.reshape(6, P).T,
                                  col(a["L0_ffn_b2"][l])], 1))

    def by_state(v):
        return np.concatenate([v.T, v.T], 0)

    la, b_, c_ = a["L0_attn_log_A"], a["L0_attn_B_param"], a["L0_attn_C_param"]
    ssm = np.concatenate([la, b_, c_, col(a["L0_attn_log_dt"]), col(a["L0_attn_D_param"]), col(a["L0_attn_ln_gamma"]),
                          col(a["L0_attn_ln_beta"]), col(a["L0_attn_b_out"]),
                          by_state(la), by_state(b_), by_state(c_),
                          np.tile(a["L0_attn_log_dt"][None, :], (P, 1)), a["L0_attn_W_out"].T], 1)
    uw, vw, ow = a["L1_attn_u_w"], a["L1_attn_v_w"], a["L1_attn_o_w"]
    heads_t0 = np.repeat(a["L1_attn_t_zero"][:, 0], 256 // HEADS)
    unit = np.concatenate([uw.T, vw.T, ow.T.reshape(2, P, DM).transpose(1, 0, 2).reshape(P, 2 * DM),
                           a["L1_attn_u_b"].reshape(2, P).T, a["L1_attn_v_b"].reshape(2, P).T,
                           heads_t0.reshape(2, P).T, col(a["L1_attn_o_b"])], 1)
    arrays = {
        "x": a["L0_attn_x"][0].T, "rot": rot, "mask": mask, "cst": cst, "wa": np.stack(wa + wa[:1]), "wm": np.stack(wm + wm[:1]),
        "ssm": ssm, "log_a_row": la.reshape(1, -1), "unit": unit,
        "mw1": a["L1_ffn_w1"].transpose(1, 0, 2),
        "mw2": a["L1_ffn_w2"].reshape(NE, MB, P, DM).transpose(2, 0, 1, 3),
        "mb1": a["L1_ffn_b1"].reshape(NE, MB, P).transpose(2, 0, 1).reshape(P, NE * MB),
        "mb2": a["L1_ffn_b2"].reshape(1, NE * DM), "mwr": a["L1_ffn_w_router"],
    }
    arrays = {f"in_{k}": np.ascontiguousarray(v) for k, v in arrays.items()}
    nc = Bacc("TRN2", target_bir_lowering=False, num_devices=1)
    ins = {k[3:]: nc.dram_tensor(k, v.shape, F32, kind="ExternalInput").ap() for k, v in arrays.items()}
    out = nc.dram_tensor("out_0", (DM, T), F32, kind="ExternalOutput").ap()
    macaron_kernel(nc, ins, out)
    r = run_bass_kernel_spmd(nc, [arrays], core_ids=[0])
    return np.ascontiguousarray(r.results[0]["out_0"].T).reshape(1, T, DM)
```

```python
from contextlib import ExitStack

import numpy as np

import concourse.bass as bass
from concourse import mybir

F32 = mybir.dt.float32
BF16 = mybir.dt.bfloat16
U32 = mybir.dt.uint32
ALU = mybir.AluOpType
ACT = mybir.ActivationFunctionType
AX = mybir.AxisListType

P = 128
T = 2048
DM = 128
C = 512
NCH = T // C
TILES = C // P
HEADS, DH, WIN = 8, 64, 64
HP = HEADS // 2
INNER = HEADS * DH
HID = int(DM * 4 * 2 / 3)
HBLK = [(0, 128), (128, 128), (256, HID - 256)]
NS = 64
L = 64
NL = T // L
NE, MH = 8, 512
MB = MH // P
VW = DH + 1
LN_EPS = 1e-5
CREDIT = 4
LN2 = float(np.log(2.0))
SS_SHIFT = 20
LOG_EXP_SET = 6


def shape_constants():
    f = np.float32
    d = np.arange(0, DH, 2, dtype=f)
    inv_freq = (f(1.0) / np.power(f(10000.0), d / f(DH))).astype(f)
    t = np.arange(T, dtype=f)
    freqs = t[:, None] * inv_freq[None, :]
    base = (d + f(0.4 * DH)) / f(1.4 * DH)
    power = (t - f(T // 2)) / f(WIN // 2)
    scale = np.power(base[None, :], power[:, None]).astype(f)
    two = lambda a: np.concatenate([a, a], 1)
    cos, sin, scale = two(np.cos(freqs)), two(np.sin(freqs)), two(scale)
    sin = sin * np.where(np.arange(DH) < DH // 2, -1.0, 1.0).astype(f)
    qk = [8.0 * cos * scale, 8.0 * sin * scale, cos / scale, sin / scale]
    rot = np.stack([np.concatenate([a.T, a.T], 0) for a in qk], 1).astype(f)

    q, k = np.arange(WIN)[:, None], np.arange(2 * WIN)[None, :]
    seen = np.where((k >= q) & (k <= q + WIN), 0.0, -1e30)
    tile = np.concatenate([np.roll(seen, WIN, 1), seen], 0)
    mask = np.tile(tile, (1, NCH * TILES))
    mask[:WIN, WIN:2 * WIN] = -1e30

    i = np.arange(P)
    ident = np.eye(P)
    centre = ident - 1.0 / DM
    mean = np.full((P, P), 1.0 / DM)
    heads = (i[:, None] // DH == i[None, :] // DH) * 1.0
    flip = ((i[:, None] < L) & (i[:, None] + i[None, :] == L - 1)) * 1.0
    taps = np.tile(L - 1.0 - np.arange(L)[None, :], (P, 1))
    decays = taps + 1.0
    back = -(L - 1.0 - i[:, None] % L)
    expert = np.tile(np.arange(NE)[None, :], (P, 1))
    cols = [ident, centre, mean, heads, flip, taps, decays, expert, back,
            np.full((P, 1), LN_EPS), np.full((P, 1), 2.0 ** (SS_SHIFT - 84)),
            np.full((P, 1), 0.5 * SS_SHIFT * LN2), np.zeros((P, 1))]
    return rot, mask.astype(f), np.concatenate(cols, 1).astype(f)


NPRM_A, NPRM_M = 4, 9
WA_COLS = 3 * INNER + HP * DM + NPRM_A
WM_COLS = 2 * HID + 3 * DM + NPRM_M
SSM_COLS = 3 * NS + 5 + 3 * DM + DM + DM
ROUTER_STEPS = 13

ROTATE, SCALE, SCORES, PROBS, VALUES = 1, 2, 3, 4, 5
PROJECT_V, FIRST_V = VALUES - 1, 2
PAIR_OUT = VALUES + 2
OUTPUT = PAIR_OUT + HEADS - 1
DRAIN = OUTPUT - HEADS + 1


def macaron_kernel(nc, ins, out, stages="FSFMUM"):
    with ExitStack() as ctx:
        arena = ctx.enter_context(nc.sbuf_tensor("arena", [P, 53200], F32))
        top = [0]

        def cols(n):
            a = arena[:, top[0]:top[0] + n]
            top[0] += n
            return a

        def sem(name):
            return ctx.enter_context(nc.semaphore(name))

        X = cols(T)
        YA, YB = cols(T + 4), cols(T + 4)
        H2 = cols(T)
        ROT = cols(4 * T).rearrange("p (k t) -> p k t", k=4)
        WA, WM = cols(WA_COLS), cols(WM_COLS)
        CST = cols(5 * P + 2 * L + NE + 5)
        MASK = cols(T // 2).bitcast(BF16)
        IDENTB = cols(P // 2).bitcast(BF16)
        R = cols(2 * NE * MH)
        SSMP = cols(SSM_COLS + 2 * DM)
        work = top[0]

        ident, centre, mean, heads_sum, flip = [CST[:, k * P:(k + 1) * P] for k in range(5)]
        o = 5 * P
        taps, decays, expert_id = CST[:, o:o + L], CST[:, o + L:o + 2 * L], CST[:, o + 2 * L:o + 2 * L + NE]
        o += 2 * L + NE
        back, eps_c, tiny_c, unshift_c, zero_c = [CST[:, o + k:o + k + 1] for k in range(5)]

        w_qkv = WA[:, 0:3 * INNER]
        w_o = WA[:, 3 * INNER:3 * INNER + HP * DM].rearrange("p (h n) -> p h n", h=HP)
        prm_a = WA[:, WA_COLS - NPRM_A:WA_COLS]
        w1 = WM[:, 0:2 * HID]
        w2 = WM[:, 2 * HID:2 * HID + 3 * DM].rearrange("p (k n) -> p k n", k=3)
        prm_m = WM[:, WM_COLS - NPRM_M:WM_COLS]

        o = 0
        parts = []
        for n in (NS, NS, NS, 1, 1, 1, 1, 1, DM, DM, DM, DM, DM, DM, DM):
            parts.append(SSMP[:, o:o + n])
            o += n
        (log_a, prm_b, prm_c, log_dt, prm_d, ln_gamma, ln_beta, b_out,
         log_a_t, prm_b_t, prm_c_t, log_dt_row, w_out, edt_row, a64_row) = parts

        HC = cols(C)
        ta, tb = cols(C), cols(C)
        rs, sq, lt, qf, pr, prt = [cols(2 * C).rearrange("p (b n) -> p b n", b=2) for _ in range(6)]
        KP = cols(2 * HP * (C + WIN)).rearrange("p (e h n) -> p e h n", e=2, h=HP)
        V = cols(TILES * HEADS * VW).rearrange("p (t h n) -> p t h n", t=TILES, h=HEADS)
        VS = cols(TILES * HEADS * VW).rearrange("p (t h n) -> p t h n", t=TILES, h=HEADS)
        ON = cols(TILES * INNER).rearrange("p (t n) -> p t n", t=TILES)
        OT = cols(HP * C).rearrange("p (h n) -> p h n", h=HP)
        mx, rec = cols(2 * TILES).rearrange("p (b n) -> p b n", b=2), cols(2 * TILES).rearrange("p (b n) -> p b n", b=2)
        assert top[0] <= 53200, top[0]

        RAW = H2[:, 0:2 * C].rearrange("p (b n) -> p b n", b=2)
        SWAP = H2[:, 2 * C:4 * C].rearrange("p (b n) -> p b n", b=2)

        top[0] = work + 9 * C
        GL, HM = [cols(3 * C).rearrange("p (k n) -> p k n", k=3) for _ in range(2)]
        a_c, cb, edt, a_t, cb_t = log_a, prm_b, log_dt, log_a_t, prm_b_t
        KTN = 16
        KT = YA[:, 0:2 * KTN * NS].rearrange("p (b t n) -> p b t n", b=2, t=KTN)
        KC = HC[:, 0:2 * L - 1]
        top[0] = work + C
        A64 = cols(DM * NL).rearrange("p (d c) -> p d c", c=NL)
        top[0] = work + 9 * C
        E = cols(DM * NS)
        UH = cols(DM * NL).rearrange("p (d c) -> p d c", c=NL)
        SS = cols(DM * NL).rearrange("p (d c) -> p d c", c=NL)
        SSO = SS.rearrange("p d c -> p (d c)")[:, 0:T]
        assert top[0] <= 53200
        YS = E[:, 0:DM * NL].rearrange("p (c d) -> p c d", d=DM)
        YT = E[:, DM * NL:DM * NL + T]
        top[0] = work + 9 * C
        HB = cols(2 * MB * C).rearrange("p (b k n) -> p b k n", b=2, k=MB)
        ACC, TMP = cols(C), cols(2 * C).rearrange("p (b n) -> p b n", b=2)
        MB1, MB2, WR = cols(NE * MB), cols(NE * DM), cols(NE)
        PB, WTS, OH, OH2, TOPV = [cols(T // P * NE).rearrange("p (t e) -> p t e", e=NE) for _ in range(5)]
        TOPI = cols(T // P * NE).bitcast(U32).rearrange("p (t e) -> p t e", e=NE)
        IDXF = cols(T // P * NE).rearrange("p (t e) -> p t e", e=NE)
        RM, RSUM = cols(T // P), cols(T // P)
        WU = cols(2 * 256 + 2 * DM + 7)
        UV = cols(8 * C).rearrange("p (b k n) -> p b k n", b=2, k=4)
        assert top[0] <= 53200

        TG = R.rearrange("p (d i) -> p d i", i=L)
        MW1 = R[:, 0:NE * MH].rearrange("p (e n) -> p e n", e=NE)
        MW2 = R[:, NE * MH:2 * NE * MH].rearrange("p (e k n) -> p e k n", e=NE, k=MB)

        bank = [ctx.enter_context(nc.psum_tensor(f"bank{i}", [P, C], F32)) for i in range(8)]
        kernel_dram = nc.dram_tensor("ssm_kernel", [P, 2 * L - 1], F32, kind="Internal")

        x_in, cst_in, rot_in, mask_in, ssm_in, kernel_out, toeplitz_in, e_in = [sem(n) for n in (
            "x_in", "cst_in", "rot_in", "mask_in", "ssm_in", "kernel_out", "toeplitz_in", "e_in")]
        wa_in, wm_in, hc_in, v_carry, v_shift, moe_w_in, moe_s_in, unit_in, x_out = [sem(n) for n in (
            "wa_in", "wm_in", "hc_in", "v_carry", "v_shift", "moe_w_in", "moe_s_in", "unit_in", "x_out")]
        table_dve, table_act, kt_prod, kt_weighed, kt_sum, kt_exp, kt_done, gt_prod, gt_exp, gt_done = [sem(n) for n in (
            "table_dve", "table_act", "kt_prod", "kt_weighed", "kt_sum", "kt_exp", "kt_done", "gt_prod", "gt_exp", "gt_done")]
        mask_done, pool_init, x_ffn, x_ssm, x_unit = [sem(n) for n in (
            "mask_done", "pool_init", "x_ffn", "x_ssm", "x_unit")]
        e_exp, e_prod, e_done, u_mm, u_evac, state_mm, state_evac, state_scan = [sem(n) for n in (
            "e_exp", "e_prod", "e_done", "u_mm", "u_evac", "state_mm", "state_evac", "state_scan")]
        y_mm, y_evac, yt_mm, yt_evac, wout_mm, ssm_sum = [sem(n) for n in (
            "y_mm", "y_evac", "yt_mm", "yt_evac", "wout_mm", "ssm_sum")]
        router_mm, router_dve, router_exp, router_top = [sem(n) for n in (
            "router_mm", "router_dve", "router_exp", "router_top")]
        rms_sq, rms_mm, rms_sqrt, rms_dve, xn_done, uv_mm, uv_silu, gated, uo_mm, unit_sum = [sem(n) for n in (
            "rms_sq", "rms_mm", "rms_sqrt", "rms_dve", "xn_done", "uv_mm", "uv_silu", "gated", "uo_mm", "unit_sum")]
        ln_cen, ln_sq, ln_var, ln_log, ln_rstd, ln_mid, ln_out = [sem("ln_" + n) for n in (
            "cen", "sq", "var", "log", "rstd", "mid", "out")]
        mlp_out, yb_ready = sem("mlp_out"), sem("yb_ready")
        copied, swap_in = sem("copied"), (sem("swap_q_in"), sem("swap_k_in"))
        proj, rotated, rot_sum, halo, no_keys, sq_done, ss_mm, ss_log, ss_rstd, unit_done = [sem(n) for n in (
            "proj", "rotated", "rot_sum", "halo", "no_keys", "sq_done", "ss_mm", "ss_log", "ss_rstd", "unit_done")]
        v_mm, v_evac, s_mm, s_max, s_sub, p_exp, pt_mm, pt_evac, o_mm, o_rec, o_norm = [sem(n) for n in (
            "v_mm", "v_evac", "s_mm", "s_max", "s_sub", "p_exp", "pt_mm", "pt_evac", "o_mm", "o_rec", "o_norm")]
        ot_mm, ot_evac, wo_mm = sem("ot_mm"), sem("ot_evac"), sem("wo_mm")
        ag_mm, gl_done, hm_done, w2_mm = sem("ag_mm"), sem("gl_done"), sem("hm_done"), sem("w2_mm")
        h_mm, h_gelu, o2_mm, o2_bias, o2_weighed, o2_acc, acc_mm, x_moe = [sem(n) for n in (
            "h_mm", "h_gelu", "o2_mm", "o2_bias", "o2_weighed", "o2_acc", "acc_mm", "x_moe")]

        def need(eng, s, n):
            eng.wait_ge(s, n + CREDIT)

        def give_credit(eng, mine):
            for s in mine:
                eng.sem_inc(s, CREDIT)

        plan, norms, seen = [], 0, {"F": 0, "S": 0, "M": 0, "U": 0}
        for kind in stages:
            plan.append((kind, norms, seen[kind]))
            norms += {"F": 3, "S": 2, "M": 1, "U": 1}[kind] * NCH
            seen[kind] += 1

        def x_whole(eng, k):
            if k == 0:
                eng.wait_ge(x_in, 16)
                return
            kind, _, run = plan[k - 1]
            if kind == "F":
                eng.wait_ge(x_ffn, run + 1)
            elif kind == "S":
                eng.wait_ge(x_ssm, NCH)
            elif kind == "M":
                need(eng, x_moe, NCH * (run + 1))
            else:
                eng.wait_ge(x_unit, NCH)

        def attention_steps(eng, call, d, step, draining=lambda t: None):
            count = 2 * NCH * call

            def run(steps, new, old, after=lambda t: None):
                for t in steps:
                    def at(k):
                        chunk = new if t >= k else old
                        return chunk and ((t - k) % HEADS,) + chunk
                    step(t, at)
                    after(t)

            run(range(HEADS), (0, d * NCH + count), None)
            with eng.Fori(0, NCH - 1) as i:
                run(range(HEADS), (i * C + C, d * NCH + i + (count + 1)), (i * C, d * NCH + i + count))
            run(range(DRAIN), None, ((NCH - 1) * C, d * NCH + (count + NCH - 1)), draining)

        def v_step(t, at):
            return at(0) and t == (PROJECT_V if at(HEADS) else FIRST_V)

        block = ctx.enter_context(nc.Block())

        @block.sync
        def _(sp):
            sp.dma_start(CST, ins["cst"]).then_inc(cst_in, 16)
            sp.dma_start(X, ins["x"]).then_inc(x_in, 16)
            sp.dma_start(WA, ins["wa"][0]).then_inc(wa_in, 16)
            sp.dma_start(ON.rearrange("p t n -> p (t n)"), ins["mask"]).then_inc(mask_in, 16)
            sp.dma_start(SSMP[:, 0:SSM_COLS], ins["ssm"]).then_inc(ssm_in, 16)
            sp.dma_start(ROT, ins["rot"]).then_inc(rot_in, 16)
            sp.dma_start(WM, ins["wm"][0]).then_inc(wm_in, 16)

            def load_experts():
                sp.dma_start(MW1, ins["mw1"]).then_inc(moe_w_in, 16)
                sp.dma_start(MW2, ins["mw2"]).then_inc(moe_w_in, 16)

            for k, (kind, norm0, run) in enumerate(plan):
                if kind == "F":
                    call = run
                    sp.wait_ge(pool_init, 3 * (call + 1))
                    need(sp, ln_out, norm0 + NCH)
                    def step(t, at):
                        if at(0):
                            u, c, g = at(0)
                            if u == 0:
                                need(sp, mlp_out, g + (1 - NCH))
                                need(sp, v_mm, g * TILES)
                                sp.dma_start(HC, YA[:, bass.ds(c, C)]).then_inc(hc_in, 16)
                            need(sp, copied, g * 8 + (u + 1))
                            for block in range(4):
                                to, frm = block * 32, (block ^ 1) * 32
                                sp.dma_start(SWAP[to:to + 32, u % 2], RAW[frm:frm + 32, u % 2]).then_inc(swap_in[u % 2], 16)

                    with sp.Fori(0, 2) as d:
                        attention_steps(sp, call, d, step)
                        need(sp, wo_mm, (d + (2 * call + 1)) * NCH)
                        sp.dma_start(WA, ins["wa"][bass.ds(d + 1, 1)].rearrange("o p n -> (o p) n")).then_inc(wa_in, 16)
                        need(sp, mlp_out, (d + (2 * call + 1)) * NCH)
                        sp.dma_start(WM, ins["wm"][bass.ds(d + 1, 1)].rearrange("o p n -> (o p) n")).then_inc(wm_in, 16)
                if kind == "S":
                    x_whole(sp, k)
                    sp.dma_start(E[0:L], ins["log_a_row"].partition_broadcast(L)).then_inc(e_in, 16)
                    sp.wait_ge(kt_done, 1)
                    sp.dma_start(kernel_dram.ap(), KC).then_inc(kernel_out, 16)
                    sp.wait_ge(kernel_out, 16)
                    sp.dma_start(TG[0:L], bass.AP(kernel_dram.ap().tensor, 0, [[1, L], [2 * L - 1, DM], [1, L]])).then_inc(toeplitz_in, 16)
                    if "M" in stages:
                        sp.wait_ge(x_ssm, NCH)
                        load_experts()
                if kind == "M":
                    if run == 0 and "S" not in stages:
                        load_experts()
                    x_whole(sp, k)
                    sp.dma_start(MB1, ins["mb1"]).then_inc(moe_s_in, 16)
                    sp.dma_start(MB2, ins["mb2"].partition_broadcast(P)).then_inc(moe_s_in, 16)
                    sp.dma_start(WR, ins["mwr"]).then_inc(moe_s_in, 16)
                if kind == "U":
                    x_whole(sp, k)
                    sp.dma_start(WU, ins["unit"]).then_inc(unit_in, 16)
            x_whole(sp, len(plan))
            sp.dma_start(out, X).then_inc(x_out, 16)
            sp.wait_ge(x_out, 16)

        @block.tensor
        def _(pe):
            mm = nc.tensor.matmul
            give_credit(pe, [ln_cen, ln_var, proj, ss_mm, v_mm, s_mm, pt_mm, o_mm, ot_mm, wo_mm,
                             ag_mm, w2_mm, h_mm, o2_mm, acc_mm])

            def centred(src, c):
                mm(bank[c][:], centre, src[:, c * C:(c + 1) * C], start=True, stop=True).then_inc(ln_cen, 1)

            def variance(n0, c):
                need(pe, ln_sq, n0 + (c + 1))
                mm(bank[4 + c][:], mean, sq[:, c % 2], start=True, stop=True).then_inc(ln_var, 1)

            def norm(src, n0, ready):
                for c in range(NCH):
                    ready(c)
                    centred(src, c)
                    if c:
                        variance(n0, c - 1)
                variance(n0, NCH - 1)

            def mlp_norm(call, d, n1, t):
                done = d * NCH + (2 * NCH * call + NCH)
                if t in (1, 2, 3):
                    c = t - 1
                    need(pe, yb_ready, d * NCH + (c + 2 * NCH * call + 1))
                    if c < 2:
                        need(pe, copied, done * 8)
                    else:
                        need(pe, ss_log, done * 8)
                    centred(YB, c)
                if t in (4, 5, 6):
                    if t == 4:
                        need(pe, s_sub, done * 8)
                    variance(n1, t - 4)
                if t == DRAIN - 1:
                    need(pe, yb_ready, done)
                    centred(YB, NCH - 1)
                    variance(n1, NCH - 1)

            def attention(call, d, n1):
                def project(u, c, g):
                    if u == 0:
                        need(pe, mlp_out, g + (1 - NCH))
                    need(pe, copied, g * 8 + (u - 1))
                    w0 = (u % 2) * INNER + (u // 2) * P
                    mm(bank[u % 2][:], w_qkv[:, w0:w0 + P], YA[:, bass.ds(c, C)], start=True, stop=True).then_inc(proj, 1)

                def project_v(c, g, first):
                    pe.wait_ge(hc_in, (g + 1) * 16)
                    for t in range(TILES):
                        if t < 2:
                            need(pe, s_sub, g * 8 + (0 if first else PROJECT_V - SCORES - 1 + t))
                        else:
                            need(pe, v_evac, g * TILES + (t - 1))
                        mm(bank[3 + (t + PROJECT_V - SCORES) % 2][:], HC[:, t * P:(t + 1) * P], w_qkv[:, 2 * INNER:],
                           start=True, stop=True).then_inc(v_mm, 1)

                def square_sum(u, c, g):
                    need(pe, sq_done, g * 8 + (u + 1))
                    need(pe, ss_log, g * 8 + u)
                    mm(bank[2][:], heads_sum, sq[:, 0], start=True, stop=True).then_inc(ss_mm, 1)

                def scores(h, c, g, first):
                    hp = h // 2
                    need(pe, unit_done, g * 8 + (2 * hp + 2))
                    need(pe, s_sub, g * 8 + (h - 1))
                    after_v = PROJECT_V - SCORES
                    if h == 0 and first:
                        need(pe, v_evac, g * TILES + TILES)
                    if after_v <= h < after_v + 2:
                        need(pe, v_evac, g * TILES + (3 + h - after_v))
                    bk = bank[3 + h % 2]
                    mm(bk[:], IDENTB, MASK[:, bass.ds(c, C)], start=True, stop=False, skip_group_check=True)
                    for w in range(2 * TILES):
                        r0, c0 = WIN * (w % 2), P * (w // 2)
                        keys = KP[:, h % 2, hp, w * WIN:w * WIN + P]
                        for to, frm in ([(0, WIN), (WIN, 0)] if w % 2 == 0 else [(0, 0)]):
                            n = WIN if w % 2 == 0 else P
                            last = mm(bk[r0:r0 + WIN, c0 + to:c0 + to + n], qf[:, hp % 2, w * WIN:(w + 1) * WIN],
                                      keys[:, frm:frm + n], start=False, stop=True, skip_group_check=True)
                    last.then_inc(s_mm, 1)

                def transpose_probs(h, c, g):
                    need(pe, p_exp, g * 8 + (h + 1))
                    need(pe, pt_evac, g * 8 + h)
                    for t in range(TILES):
                        last = nc.tensor.transpose(bank[5][:, t * P:(t + 1) * P], pr[:, h % 2, t * P:(t + 1) * P], ident)
                    last.then_inc(pt_mm, 1)

                def values(h, c, g):
                    need(pe, pt_evac, g * 8 + (h + 1))
                    need(pe, o_norm, g * 8 + h)
                    if h == 0:
                        need(pe, v_carry, 2 * g + 2)
                        need(pe, v_shift, g + 1)
                    for w in range(2 * TILES):
                        t, r0 = w // 2, WIN * (w % 2)
                        last = mm(bank[6][r0:r0 + WIN, t * VW:(t + 1) * VW], prt[:, h % 2, w * WIN:(w + 1) * WIN],
                                  (VS if w % 2 == 0 else V)[:, t, h, :], start=True, stop=True)
                    last.then_inc(o_mm, 1)

                def transpose_out(hp, g):
                    need(pe, o_norm, g * 8 + (2 * hp + 2))
                    if hp:
                        need(pe, ot_evac, g * HP + hp)
                    else:
                        need(pe, yb_ready, g)
                    for t in range(TILES):
                        last = nc.tensor.transpose(bank[7][:, t * P:(t + 1) * P], ON[:, t, hp * P:(hp + 1) * P], ident)
                    last.then_inc(ot_mm, 1)

                def output(g):
                    need(pe, ot_evac, g * HP + HP)
                    for hp in range(HP):
                        last = mm(bank[7][:], w_o[:, hp], OT[:, hp], start=(hp == 0), stop=(hp == HP - 1))
                    last.then_inc(wo_mm, 1)

                def step(t, at):
                    if at(0):
                        project(*at(0))
                    if at(VALUES):
                        values(*at(VALUES))
                    if v_step(t, at):
                        project_v(*at(0)[1:], first=not at(HEADS))
                    if at(0):
                        square_sum(*at(0))
                    if at(PAIR_OUT) and at(PAIR_OUT)[0] % 2 == 0:
                        transpose_out(at(PAIR_OUT)[0] // 2, at(PAIR_OUT)[2])
                    if at(SCORES):
                        scores(*at(SCORES), first=not at(HEADS))
                    if at(PROBS):
                        transpose_probs(*at(PROBS))
                    if t == OUTPUT - HEADS and at(HEADS):
                        output(at(HEADS)[2])

                pe.wait_ge(wa_in, (d + (2 * call + 1)) * 16)
                attention_steps(pe, call, d, step, lambda t: mlp_norm(call, d, n1, t))

            def mlp(call, d, n1):
                def hidden(j, c, g):
                    k0, m = HBLK[j]
                    need(pe, hm_done, g * 3 + (j - 2))
                    for half in range(2):
                        last = mm(bank[2 * j + half][0:m, :], w1[:, half * HID + k0:half * HID + k0 + m],
                                  H2[:, bass.ds(c, C)], start=True, stop=True)
                    last.then_inc(ag_mm, 1)

                def output(j, g):
                    need(pe, hm_done, g * 3 + (j + 1))
                    if j == 0:
                        need(pe, mlp_out, g)
                    mm(bank[7][:], w2[0:HBLK[j][1], j], HM[0:HBLK[j][1], j], start=(j == 0), stop=(j == 2)).then_inc(w2_mm, 1)

                g0 = d * NCH + 2 * NCH * call
                pe.wait_ge(wm_in, (d + (2 * call + 1)) * 16)
                need(pe, ln_out, n1 + NCH)
                for j in range(3):
                    hidden(j, 0, g0)
                with pe.Fori(0, NCH - 1) as i:
                    g = d * NCH + i + 2 * NCH * call
                    for j in range(3):
                        hidden(j, i * C + C, g + 1)
                        output(j, g)
                for j in range(3):
                    output(j, g0 + (NCH - 1))

            def ssm(norm0):
                need(pe, ln_out, norm0 + 2 * NCH)
                for q in range(8):
                    if q >= 4:
                        pe.wait_ge(u_evac, q - 3)
                    for k in range(4):
                        c = 4 * q + k
                        last = nc.tensor.transpose(bank[q % 4][0:L, k * P:(k + 1) * P], H2[:, c * L:(c + 1) * L], ident)
                    last.then_inc(u_mm, 1)
                pe.wait_ge(u_evac, 8)
                for q in range(8):
                    if q % 2 == 0:
                        pe.wait_ge(e_done, q // 2 + 1)
                    if q >= 4:
                        pe.wait_ge(state_evac, q - 3)
                    for k in range(16):
                        dd = 16 * q + k
                        last = mm(bank[4 + q % 4][L:P, k * NL:(k + 1) * NL], E[0:L, dd * NS:(dd + 1) * NS], UH[0:L, dd, :], start=True, stop=True)
                    last.then_inc(state_mm, 1)
                pe.wait_ge(toeplitz_in, 16)
                pe.wait_ge(gt_done, 4)
                for q in range(8):
                    if q % 4 == 0:
                        pe.wait_ge(state_scan, q // 4 + 1)
                    if q >= 4:
                        pe.wait_ge(y_evac, q - 3)
                    for k in range(16):
                        dd = 16 * q + k
                        last = mm(bank[q % 4][0:L, k * NL:(k + 1) * NL], TG[:, dd, :], UH[:, dd, :], start=True, stop=True)
                    last.then_inc(y_mm, 1)
                pe.wait_ge(y_evac, 8)
                for q in range(NCH):
                    for k in range(8):
                        last = mm(bank[4 + q][:, k * L:(k + 1) * L], YS[0:L, 8 * q + k, :], flip[0:L, 0:L], start=True, stop=True)
                    last.then_inc(yt_mm, 1)
                for q in range(NCH):
                    pe.wait_ge(yt_evac, q + 1)
                    mm(bank[q][:], w_out, YT[:, q * C:(q + 1) * C], start=True, stop=True).then_inc(wout_mm, 1)

            def mixture(norm0, moe):
                pe.wait_ge(moe_w_in, 32)
                pe.wait_ge(moe_s_in, 48 * (moe + 1))
                need(pe, ln_out, norm0 + NCH)
                for t in range(T // P):
                    last = mm(bank[7][:, t * NE:(t + 1) * NE], YB[:, t * P:(t + 1) * P], WR, start=True, stop=True)
                last.then_inc(router_mm, 1)

                def hidden(e, c, g):
                    for j in range(MB):
                        need(pe, h_gelu, g * (NE * MB) + (e * MB + j - MB + 1))
                        mm(bank[j][:], MW1[:, e, j * P:(j + 1) * P], YB[:, bass.ds(c, C)], start=True, stop=True).then_inc(h_mm, 1)

                def expert_out(e, g):
                    need(pe, h_gelu, g * (NE * MB) + (e + 1) * MB)
                    need(pe, o2_bias, g * NE + (e - 1))
                    for t in range(TILES):
                        for j in range(MB):
                            last = mm(bank[4 + e % 2][:, t * P:(t + 1) * P], HB[:, e % 2, j, t * P:(t + 1) * P], MW2[:, e, j],
                                      start=(j == 0), stop=(j == MB - 1))
                    last.then_inc(o2_mm, 1)

                def transpose_sum(g):
                    need(pe, o2_acc, g * NE + NE)
                    need(pe, x_moe, g)
                    for t in range(TILES):
                        last = nc.tensor.transpose(bank[6][:, t * P:(t + 1) * P], ACC[:, t * P:(t + 1) * P], ident)
                    last.then_inc(acc_mm, 1)

                def chunk(c, g, before):
                    for e in range(NE):
                        hidden(e, c, g)
                        if e > 0:
                            if e == 1 and before is not None:
                                transpose_sum(before)
                            expert_out(e - 1, g)
                        elif before is not None:
                            expert_out(NE - 1, before)

                chunk(0, NCH * moe, None)
                with pe.Fori(0, NCH - 1) as i:
                    chunk(i * C + C, i + (NCH * moe + 1), i + NCH * moe)
                expert_out(NE - 1, NCH * moe + NCH - 1)
                transpose_sum(NCH * moe + NCH - 1)

            def unit(norm0):
                pe.wait_ge(unit_in, 16)
                for c in range(NCH):
                    pe.wait_ge(rms_sq, c + 1)
                    if c >= 2:
                        pe.wait_ge(rms_sqrt, c - 1)
                    mm(bank[6 + c % 2][:], mean, sq[:, c % 2], start=True, stop=True).then_inc(rms_mm, 1)
                for c in range(NCH + 1):
                    if c < NCH:
                        pe.wait_ge(xn_done, c + 1)
                        for k in range(4):
                            if c:
                                pe.wait_ge(uv_silu, 4 * (c - 1) + k + 1)
                            mm(bank[k][:], WU[:, k * P:(k + 1) * P], H2[:, c * C:(c + 1) * C], start=True, stop=True).then_inc(uv_mm, 1)
                    if c:
                        pe.wait_ge(gated, 2 * c)
                        if c >= 3:
                            pe.wait_ge(unit_sum, c - 2)
                        for k in range(2):
                            last = mm(bank[4 + (c - 1) % 2][:], WU[:, 4 * P + k * P:4 * P + (k + 1) * P], UV[:, (c - 1) % 2, k],
                                      start=(k == 0), stop=(k == 1))
                        last.then_inc(uo_mm, 1)

            pe.wait_ge(cst_in, 16)
            for k, (kind, norm0, run) in enumerate(plan):
                x_whole(pe, k)
                norm(X, norm0, lambda c: None)
                if kind == "F":
                    need(pe, ln_out, norm0 + NCH)
                    pe.wait_ge(mask_done, 1)
                    with pe.Fori(0, 2) as d:
                        n1 = d * NCH + (norm0 + NCH)
                        attention(run, d, n1)
                        mlp(run, d, n1)
                elif kind == "S":
                    norm(YB, norm0 + NCH, lambda c: need(pe, ln_out, c + (norm0 + 1)))
                    ssm(norm0)
                elif kind == "M":
                    mixture(norm0, run)
                elif kind == "U":
                    unit(norm0)

        @block.scalar
        def _(act):
            A = nc.scalar.activation
            give_credit(act, [v_carry, ln_sq, ln_log, ln_rstd, copied, sq_done, ss_log, ss_rstd, v_evac, p_exp, pt_evac,
                              ot_evac, gl_done, h_gelu])

            def log_exp_table():
                act.add_instruction(mybir.InstLoadActFuncSet(
                    act_func_set_id=LOG_EXP_SET, name=nc.get_next_instruction_name(),
                    engine=mybir.EngineType.Activation))

            def norm_square(n0, c):
                need(act, ln_cen, n0 + (c + 1))
                need(act, ln_var, n0 + (c - 1))
                A(sq[:, c % 2], bank[c][:], ACT.Square).then_inc(ln_sq, 1)

            def norm_root(n0, c):
                need(act, ln_var, n0 + (c + 1))
                need(act, ln_rstd, n0 + (c - 1))
                A(lt[:, c % 2], bank[4 + c][:], ACT.Ln, bias=eps_c).then_inc(ln_log, 1)
                need(act, ln_log, n0 + (c + 1))
                need(act, ln_out, n0 + (c - 1))
                A(rs[:, c % 2], lt[:, c % 2], ACT.Exp, scale=-0.5, bias=zero_c).then_inc(ln_rstd, 1)

            def norm(n0):
                for c in range(NCH):
                    norm_square(n0, c)
                    if c:
                        norm_root(n0, c - 1)
                norm_root(n0, NCH - 1)

            def mlp_norm(call, d, n1, t):
                if t in (2, 3):
                    norm_square(n1, t - 2)
                if t == 5:
                    need(act, unit_done, (d * NCH + (2 * NCH * call + NCH)) * 8)
                    norm_root(n1, 0)
                    norm_square(n1, 2)
                if t == 6:
                    norm_root(n1, 1)
                    norm_root(n1, 2)
                    norm_square(n1, 3)
                    norm_root(n1, 3)

            def attention(call, d, n1):
                def square(u, c, g):
                    need(act, proj, g * 8 + (u + 1))
                    need(act, rotated, g * 8 + (u - 1))
                    A(sq[:, 0], bank[u % 2][:], ACT.Square).then_inc(sq_done, 1)
                    A(RAW[:, u % 2], bank[u % 2][:], ACT.Copy).then_inc(copied, 1)

                def evacuate_v(c, g):
                    need(act, o_mm, g * 8)
                    A(VS[WIN:P, 0], V[WIN:P, TILES - 1], ACT.Copy).then_inc(v_carry, 1)
                    for t in range(TILES):
                        need(act, v_mm, g * TILES + (t + 1))
                        if t == TILES - 1:
                            need(act, v_carry, 2 * g + 1)
                        A(V[:, t, :, 0:DH], bank[3 + (t + PROJECT_V - SCORES) % 2][:].rearrange("p (h n) -> p h n", h=HEADS),
                          ACT.Copy).then_inc(v_evac, 1)
                    need(act, v_evac, g * TILES + TILES - 1)
                    A(VS[WIN:P, 1:TILES], V[WIN:P, 0:TILES - 1], ACT.Copy).then_inc(v_carry, 1)

                def inverse_norm(u, c, g):
                    need(act, ss_mm, g * 8 + (u + 1))
                    A(lt[:, 0], bank[2][:], ACT.Ln, scale=2.0 ** SS_SHIFT, bias=tiny_c).then_inc(ss_log, 1)
                    need(act, ss_log, g * 8 + (u + 1))
                    need(act, unit_done, g * 8 + (u - 1))
                    A(rs[:, u % 2], lt[:, 0], ACT.Exp, scale=-0.5, bias=unshift_c).then_inc(ss_rstd, 1)

                def exp(h, c, g):
                    need(act, s_sub, g * 8 + (h + 1))
                    A(pr[:, h % 2], pr[:, h % 2], ACT.Exp, bias=zero_c).then_inc(p_exp, 1)

                def evacuate_probs(h, c, g):
                    need(act, pt_mm, g * 8 + (h + 1))
                    A(prt[:, h % 2], bank[5][:], ACT.Copy).then_inc(pt_evac, 1)

                def evacuate_out(hp, g):
                    need(act, ot_mm, g * HP + (hp + 1))
                    A(OT[:, hp], bank[7][:], ACT.Copy).then_inc(ot_evac, 1)

                def step(t, at):
                    if at(0):
                        square(*at(0))
                    if at(PROBS):
                        exp(*at(PROBS))
                    if v_step(t, at):
                        evacuate_v(*at(0)[1:])
                    if at(0):
                        inverse_norm(*at(0))
                    if at(PAIR_OUT) and at(PAIR_OUT)[0] % 2 == 0:
                        evacuate_out(at(PAIR_OUT)[0] // 2, at(PAIR_OUT)[2])
                    if at(PROBS):
                        evacuate_probs(*at(PROBS))

                attention_steps(act, call, d, step, lambda t: mlp_norm(call, d, n1, t))

            def mlp(call, d):
                with act.Fori(0, NCH) as i:
                    g = d * NCH + i + 2 * NCH * call
                    for j, (k0, m) in enumerate(HBLK):
                        need(act, ag_mm, g * 3 + (j + 1))
                        A(GL[0:m, j], bank[2 * j + 1][0:m, :], ACT.Gelu, bias=prm_m[0:m, 5 + j:6 + j]).then_inc(gl_done, 1)

            def small_tables():
                act.wait_ge(ssm_in, 16)
                A(a_c, log_a, ACT.Exp, bias=zero_c).then_inc(table_act, 1)
                A(edt, log_dt, ACT.Exp, bias=zero_c).then_inc(table_act, 1)
                A(a_t[L:P], log_a_t[L:P], ACT.Exp, bias=zero_c[L:P]).then_inc(table_act, 1)
                A(edt_row, log_dt_row, ACT.Exp, bias=zero_c).then_inc(table_act, 1)

            def decays_exp():
                for q in range(4):
                    act.wait_ge(gt_prod, q + 1)
                    v = TG[L:P, 32 * q:32 * q + 32, :]
                    A(v, v, ACT.Exp, bias=zero_c[L:P]).then_inc(gt_exp, 1)

            def tables():
                for b in range(L // KTN):
                    act.wait_ge(kt_prod, b + 1)
                    A(KT[:, b % 2], KT[:, b % 2], ACT.Exp, bias=zero_c).then_inc(kt_exp, 1)

            def ssm(norm0):
                A(a64_row[L:P], a_t[L:P], ACT.Exp, scale=float(L), bias=zero_c[L:P]).then_inc(table_act, 1)
                act.wait_ge(e_in, 16)
                q4 = DM * NS // 4
                for q in range(4):
                    v = E[0:L, q * q4:(q + 1) * q4]
                    A(v, v, ACT.Exp, bias=zero_c[0:L]).then_inc(e_exp, 1)
                for q in range(4):
                    v = E[0:L, q * q4:(q + 1) * q4]
                    act.wait_ge(e_prod, q + 1)
                    A(v, v, ACT.Exp, scale=back[0:L], bias=zero_c[0:L]).then_inc(e_done, 1)
                for q in range(8):
                    act.wait_ge(u_mm, q + 1)
                    A(UH[0:L, :, 4 * q:4 * q + 4], bank[q % 4][0:L, :].rearrange("p (c d) -> p d c", d=DM),
                      ACT.Copy).then_inc(u_evac, 1)
                tables()
                act.wait_ge(state_mm, 8)
                for q in range(8):
                    act.wait_ge(y_mm, q + 1)
                    A(YS[0:L, :, 16 * q:16 * q + 16], bank[q % 4][0:L, :].rearrange("p (d c) -> p c d", c=NL),
                      ACT.Copy).then_inc(y_evac, 1)
                for q in range(NCH):
                    act.wait_ge(yt_mm, q + 1)
                    A(YT[:, q * C:(q + 1) * C], bank[4 + q][:], ACT.Copy).then_inc(yt_evac, 1)

            def mixture(moe):
                act.wait_ge(moe_s_in, 48 * (moe + 1))
                act.wait_ge(router_dve, ROUTER_STEPS * moe + 2)
                A(PB, PB, ACT.Exp, bias=zero_c).then_inc(router_exp, 1)
                with act.Fori(0, NCH) as i:
                    g = i + NCH * moe
                    for e in range(NE):
                        need(act, o2_mm, g * NE + (e - 1))
                        for j in range(MB):
                            need(act, h_mm, g * (NE * MB) + (e * MB + j + 1))
                            A(HB[:, e % 2, j], bank[j][:], ACT.Gelu_apprx_tanh,
                              bias=MB1[:, e * MB + j:e * MB + j + 1]).then_inc(h_gelu, 1)

            def unit(norm0):
                act.wait_ge(unit_in, 16)
                need(act, ln_out, norm0 + NCH)
                for c in range(NCH):
                    if c >= 2:
                        act.wait_ge(rms_mm, c - 1)
                    A(sq[:, c % 2], YB[:, c * C:(c + 1) * C], ACT.Square).then_inc(rms_sq, 1)
                for c in range(NCH):
                    act.wait_ge(rms_mm, c + 1)
                    A(H2[:, c * C:(c + 1) * C], bank[6 + c % 2][:], ACT.Sqrt, bias=zero_c).then_inc(rms_sqrt, 1)
                for c in range(NCH):
                    if c >= 2:
                        act.wait_ge(uo_mm, c - 1)
                    for k in range(4):
                        act.wait_ge(uv_mm, 4 * c + k + 1)
                        A(UV[:, c % 2, k], bank[k][:], ACT.Silu, bias=WU[:, 6 * P + k:6 * P + k + 1]).then_inc(uv_silu, 1)

            act.wait_ge(cst_in, 16)
            log_exp_table()
            for k, (kind, norm0, run) in enumerate(plan):
                if kind == "S" and k:
                    decays_exp()
                norm(norm0)
                if k == 0:
                    small_tables()
                if kind == "S" and k == 0:
                    decays_exp()
                if kind == "F":
                    with act.Fori(0, 2) as d:
                        attention(run, d, d * NCH + (norm0 + NCH))
                        mlp(run, d)
                        log_exp_table()
                elif kind == "S":
                    norm(norm0 + NCH)
                    ssm(norm0)
                elif kind == "M":
                    mixture(run)
                    log_exp_table()
                elif kind == "U":
                    unit(norm0)
                    log_exp_table()

        @block.vector
        def _(dve):
            TT = nc.vector.tensor_tensor
            STT = nc.vector.scalar_tensor_tensor
            give_credit(dve, [v_shift, ln_mid, ln_out, mlp_out, yb_ready, rotated, unit_done, s_max, s_sub, o_rec, o_norm,
                              hm_done, o2_bias, o2_weighed, o2_acc, x_moe])
            halves = ((0, DH, 0), (DH, P, 1))

            def wide(v, n):
                return v.unsqueeze(2).to_broadcast([v.shape[0], v.shape[1], n])

            def across(v, n):
                return v.unsqueeze(1).to_broadcast([v.shape[0], n, v.shape[1]])

            def small_tables():
                dve.wait_ge(ssm_in, 16)
                TT(cb, prm_c, prm_b, ALU.mult).then_inc(table_dve, 1)
                TT(cb_t[L:P], prm_c_t[L:P], prm_b_t[L:P], ALU.mult).then_inc(table_dve, 1)
                dve.wait_ge(table_dve, 2)
                dve.wait_ge(table_act, 4)
                nc.vector.tensor_scalar(a_c, a_c, edt, -1.0, ALU.mult, ALU.mult).then_inc(table_dve, 1)
                nc.vector.tensor_scalar(cb, cb, edt, None, ALU.mult).then_inc(table_dve, 1)
                STT(out=a_t[L:P], in0=a_t[L:P], scalar=-1.0, in1=edt_row[L:P], op0=ALU.mult, op1=ALU.mult).then_inc(table_dve, 1)
                TT(cb_t[L:P], cb_t[L:P], edt_row[L:P], ALU.mult).then_inc(table_dve, 1)

            def tables():
                nc.vector.memset(KC[:, L:2 * L - 1], 0.0)
                taps_at = lambda b: slice(KTN * b, KTN * b + KTN)

                for b in range(L // KTN + 1):
                    if b < L // KTN:
                        if b >= 2:
                            dve.wait_ge(kt_sum, b - 1)
                        TT(KT[:, b % 2], wide(taps[:, taps_at(b)], NS), across(a_c, KTN), ALU.mult).then_inc(kt_prod, 1)
                    if b:
                        v = KT[:, (b - 1) % 2]
                        dve.wait_ge(kt_exp, b)
                        TT(v, v, across(cb, KTN), ALU.mult).then_inc(kt_weighed, 1)
                        dve.wait_ge(kt_weighed, b)
                        nc.vector.tensor_reduce(KC[:, taps_at(b - 1)], v, AX.X, ALU.add).then_inc(kt_sum, 1)
                dve.wait_ge(kt_sum, L // KTN)
                TT(KC[:, L - 1:L], KC[:, L - 1:L], prm_d, ALU.add).then_inc(kt_done, 1)

            def norm_chunks(n0, write, chunks=range(NCH)):
                for c in chunks:
                    need(dve, ln_rstd, n0 + (c + 1))
                    write(c, n0 + c)

            def plain(c, n):
                TT(YB[:, c * C:(c + 1) * C], bank[c][:], rs[:, c % 2], ALU.mult).then_inc(ln_out, 1)

            def shifted(c, n):
                for p0, p1, shift in halves:
                    last = TT(YA[p0:p1, c * C + shift:(c + 1) * C + shift], bank[c][p0:p1, :], rs[p0:p1, c % 2], ALU.mult)
                last.then_inc(ln_out, 1)

            def affine(gain, bias):
                def write(c, n):
                    buf = (ta, tb)[c % 2]
                    if c >= 2:
                        need(dve, ln_out, n - 1)
                    TT(buf, bank[c][:], rs[:, c % 2], ALU.mult).then_inc(ln_mid, 1)
                    need(dve, ln_mid, n_mid[0] + n)
                    nc.vector.tensor_scalar(H2[:, c * C:(c + 1) * C], buf, gain, bias, ALU.mult, ALU.add).then_inc(ln_out, 1)
                return write

            def attention(call, d, draining):
                def rotate(u, c, g):
                    k = u % 2
                    chunk = bass.ds(c, C)
                    dve.wait_ge(swap_in[k], (g * HP + (u // 2 + 1)) * 64)
                    STT(out=tb, in0=SWAP[:, k], scalar=prm_a[:, 2 * k + 1:2 * k + 2], in1=ROT[:, 2 * k + 1, chunk],
                        op0=ALU.mult, op1=ALU.mult)
                    need(dve, unit_done, g * 8 + u)
                    STT(out=ta, in0=RAW[:, k], scalar=prm_a[:, 2 * k:2 * k + 1], in1=ROT[:, 2 * k, chunk],
                        op0=ALU.mult, op1=ALU.mult).then_inc(rotated, 1)

                def normalise(u, c, g):
                    hp = u // 2
                    need(dve, ss_rstd, g * 8 + (u + 1))
                    need(dve, rot_sum, g * 8 + (u + 1))
                    if u % 2 == 0:
                        last = STT(out=qf[:, hp % 2], in0=rs[:, 0], scalar=1e12, in1=ta, op0=ALU.min, op1=ALU.mult)
                    else:
                        need(dve, halo, g * HP + (hp + 1))
                        for e in range(2):
                            p0, p1 = e * DH, (e + 1) * DH
                            last = STT(out=KP[p0:p1, e, hp, WIN:WIN + C], in0=rs[p0:p1, 1], scalar=1e12,
                                       in1=ta[p0:p1], op0=ALU.min, op1=ALU.mult)
                    last.then_inc(unit_done, 1)

                def softmax(h, c, g):
                    by_row = lambda a: a.rearrange("p (t k) -> p t k", t=TILES)
                    need(dve, s_mm, g * 8 + (h + 1))
                    nc.vector.tensor_reduce(mx[:, h % 2], by_row(bank[3 + h % 2][:]), AX.X, ALU.max).then_inc(s_max, 1)
                    need(dve, s_max, g * 8 + (h + 1))
                    TT(by_row(pr[:, h % 2]), by_row(bank[3 + h % 2][:]), wide(mx[:, h % 2], P), ALU.subtract).then_inc(s_sub, 1)

                def divide(h, c, g):
                    o = bank[6][:, 0:TILES * VW].rearrange("p (t n) -> p t n", n=VW)
                    need(dve, o_mm, g * 8 + (h + 1))
                    nc.vector.reciprocal(rec[:, h % 2].unsqueeze(2), o[:, :, DH:VW]).then_inc(o_rec, 1)
                    need(dve, o_rec, g * 8 + (h + 1))
                    TT(ON[:, :, h * DH:(h + 1) * DH], o[:, :, 0:DH], wide(rec[:, h % 2], DH), ALU.mult).then_inc(o_norm, 1)

                def residual(c, g):
                    need(dve, wo_mm, g + 1)
                    for p0, p1, shift in halves:
                        to = bass.ds(c + shift, C)
                        last = TT(YB[p0:p1, to], bank[7][p0:p1, :], YA[p0:p1, to], ALU.add)
                    last.then_inc(yb_ready, 1)

                def step(t, at):
                    if at(SCORES + 1):
                        softmax(*at(SCORES + 1))
                    if at(SCALE):
                        normalise(*at(SCALE))
                    if at(ROTATE):
                        rotate(*at(ROTATE))
                    if at(VALUES):
                        divide(*at(VALUES))
                    if v_step(t, at):
                        g = at(0)[2]
                        need(dve, v_evac, g * TILES + TILES)
                        nc.vector.tensor_scalar(VS[0:WIN], V[0:WIN], 1.0, None, ALU.mult).then_inc(v_shift, 1)
                    if t == OUTPUT - HEADS and at(HEADS):
                        residual(*at(HEADS)[1:])

                dve.wait_ge(wa_in, (d + (2 * call + 1)) * 16)
                attention_steps(dve, call, d, step, draining)

            def mlp(call, d):
                def gate(c, g):
                    for j, (k0, m) in enumerate(HBLK):
                        need(dve, gl_done, g * 3 + (j + 1))
                        need(dve, w2_mm, g * 3 + (j - 2))
                        STT(out=HM[0:m, j], in0=bank[2 * j][0:m, :], scalar=prm_m[0:m, 2 + j:3 + j], in1=GL[0:m, j],
                            op0=ALU.add, op1=ALU.mult).then_inc(hm_done, 1)

                def residual(c, g):
                    need(dve, w2_mm, g * 3 + 3)
                    for p0, p1, shift in halves:
                        to = bass.ds(c + shift, C)
                        last = STT(out=YA[p0:p1, to], in0=bank[7][p0:p1, :], scalar=prm_m[p0:p1, 8:9], in1=YB[p0:p1, to],
                                   op0=ALU.add, op1=ALU.add)
                    last.then_inc(mlp_out, 1)

                g0 = d * NCH + 2 * NCH * call
                gate(0, g0)
                with dve.Fori(0, NCH - 1) as i:
                    g = d * NCH + i + 2 * NCH * call
                    gate(i * C + C, g + 1)
                    residual(i * C, g)
                residual((NCH - 1) * C, g0 + (NCH - 1))

            def ssm(norm0):
                need(dve, ln_out, norm0 + 2 * NCH)
                dve.wait_ge(table_act, 5)
                nc.vector.tensor_copy(A64[L:P], wide(a64_row[L:P], NL)).then_inc(ssm_sum, 1)
                dve.wait_ge(ssm_sum, 1)
                nc.vector.memset(A64[L:P, :, 0:1], 0.0).then_inc(ssm_sum, 1)
                nc.vector.memset(SS[L:P, :, 0:1], 0.0).then_inc(ssm_sum, 1)
                for q in range(4):
                    dve.wait_ge(e_exp, q + 1)
                    v = E[0:L, q * (DM * NS // 4):(q + 1) * (DM * NS // 4)].rearrange("p (d n) -> p d n", n=NS)
                    TT(v, v, wide(edt_row[0:L, 32 * q:32 * q + 32], NS), ALU.mult).then_inc(e_prod, 1)
                tables()
                for q in range(8):
                    dve.wait_ge(state_mm, q + 1)
                    nc.vector.tensor_copy(SS[L:P, 16 * q:16 * q + 16, 1:NL],
                                          bank[4 + q % 4][L:P, :].rearrange("p (d c) -> p d c", c=NL)[:, :, 0:NL - 1]).then_inc(state_evac, 1)
                    if q % 4 == 3:
                        dve.wait_ge(state_evac, q + 1)
                        dve.wait_ge(ssm_sum, 3)
                        flat = lambda a: a[L:P, 64 * (q // 4):64 * (q // 4) + 64, :].rearrange("p d c -> p (d c)")
                        nc.vector.tensor_tensor_scan(flat(UH), flat(A64), flat(SS), 0.0, ALU.mult, ALU.add).then_inc(state_scan, 1)
                for q in range(NCH):
                    c = slice(q * C, (q + 1) * C)
                    dve.wait_ge(wout_mm, q + 1)
                    STT(out=SSO[:, c], in0=bank[q][:], scalar=b_out, in1=YB[:, c], op0=ALU.add, op1=ALU.add).then_inc(ssm_sum, 1)
                    dve.wait_ge(ssm_sum, 4 + q)
                    TT(X[:, c], X[:, c], SSO[:, c], ALU.add).then_inc(x_ssm, 1)

            def mixture(moe):
                n = [ROUTER_STEPS * moe]

                def chained(instruction):
                    instruction.then_inc(router_dve, 1)
                    n[0] += 1
                    dve.wait_ge(router_dve, n[0])

                rt = bank[7][:, 0:T // P * NE].rearrange("p (t e) -> p t e", e=NE)
                dve.wait_ge(router_mm, moe + 1)
                chained(nc.vector.tensor_reduce(RM, rt, AX.X, ALU.max))
                chained(TT(PB, rt, wide(RM, NE), ALU.subtract))
                dve.wait_ge(router_exp, moe + 1)
                chained(nc.vector.tensor_reduce(RSUM, PB, AX.X, ALU.add))
                chained(nc.vector.reciprocal(RSUM, RSUM))
                chained(TT(PB, PB, wide(RSUM, NE), ALU.mult))
                for t in range(T // P):
                    last = nc.vector.max(TOPV[:, t], PB[:, t])
                chained(last)
                for t in range(T // P):
                    last = nc.vector.max_index(TOPI[:, t], TOPV[:, t], PB[:, t])
                chained(last)
                chained(nc.vector.tensor_copy(IDXF, TOPI))
                for k, oh in enumerate((WTS, OH)):
                    chained(TT(oh, across(expert_id, T // P), IDXF[:, :, k:k + 1].to_broadcast([P, T // P, NE]), ALU.is_equal))
                    chained(TT(oh, oh, TOPV[:, :, k:k + 1].to_broadcast([P, T // P, NE]), ALU.mult))
                chained(TT(WTS, WTS, OH, ALU.add))
                assert n[0] == ROUTER_STEPS * (moe + 1)
                with dve.Fori(0, NCH) as i:
                    g = i + NCH * moe
                    tiles = lambda a: a.rearrange("p (t n) -> p t n", t=TILES)
                    for e in range(NE):
                        tmp = TMP[:, e % 2]
                        need(dve, o2_mm, g * NE + (e + 1))
                        TT(tiles(tmp), tiles(bank[4 + e % 2][:]), across(MB2[:, e * DM:(e + 1) * DM], TILES), ALU.add).then_inc(o2_bias, 1)
                        need(dve, o2_bias, g * NE + (e + 1))
                        w = WTS[:, bass.ds(i * TILES, TILES), e:e + 1].to_broadcast([P, TILES, DM])
                        if e == 0:
                            need(dve, acc_mm, g)
                        TT(tiles(tmp if e else ACC), tiles(tmp), w, ALU.mult).then_inc(o2_weighed if e else o2_acc, 1)
                        if e:
                            need(dve, o2_weighed, g * (NE - 1) + e)
                            TT(ACC, ACC, tmp, ALU.add).then_inc(o2_acc, 1)
                        need(dve, o2_acc, g * NE + (e + 1))
                    need(dve, acc_mm, g + 1)
                    c = bass.ds(i * C, C)
                    STT(out=X[:, c], in0=bank[6][:], scalar=0.5, in1=X[:, c], op0=ALU.mult, op1=ALU.add).then_inc(x_moe, 1)

            def unit():
                for c in range(NCH):
                    r = H2[:, c * C:(c + 1) * C]
                    dve.wait_ge(rms_sqrt, c + 1)
                    nc.vector.tensor_scalar(r, r, 1e-8, None, ALU.add).then_inc(rms_dve, 1)
                    dve.wait_ge(rms_dve, 2 * c + 1)
                    nc.vector.reciprocal(r, r).then_inc(rms_dve, 1)
                    dve.wait_ge(rms_dve, 2 * c + 2)
                    TT(r, YB[:, c * C:(c + 1) * C], r, ALU.mult).then_inc(xn_done, 1)
                for c in range(NCH + 1):
                    if c < NCH:
                        dve.wait_ge(uv_silu, 4 * c + 4)
                        for k in range(2):
                            STT(out=UV[:, c % 2, k], in0=UV[:, c % 2, k], scalar=WU[:, 6 * P + 4 + k:6 * P + 5 + k],
                                in1=UV[:, c % 2, 2 + k], op0=ALU.mult, op1=ALU.mult).then_inc(gated, 1)
                    if c:
                        cc, b = slice((c - 1) * C, c * C), (c - 1) % 2
                        dve.wait_ge(uo_mm, c)
                        STT(out=lt[:, b], in0=bank[4 + b][:], scalar=WU[:, 6 * P + 6:6 * P + 7], in1=YB[:, cc],
                            op0=ALU.add, op1=ALU.add).then_inc(unit_sum, 1)
                        dve.wait_ge(unit_sum, c)
                        TT(X[:, cc], X[:, cc], lt[:, b], ALU.add).then_inc(x_unit, 1)

            dve.wait_ge(cst_in, 16)
            affines = 0
            for k, (kind, norm0, run) in enumerate(plan):
                if kind == "F":
                    nc.vector.memset(YA[DH:P, 0:1], 0.0)
                norm_chunks(norm0, shifted if kind == "F" else plain)
                if k == 0:
                    dve.wait_ge(mask_in, 16)
                    nc.vector.tensor_copy(MASK, ON.rearrange("p t n -> p (t n)"))
                    nc.vector.tensor_copy(IDENTB, ident).then_inc(mask_done, 1)
                    small_tables()
                    dve.wait_ge(rot_in, 16)
                if kind == "F":
                    n_mid = [affines + 1 - (norm0 + NCH)]
                    nc.vector.memset(YB[DH:P, 0:1], 0.0)
                    with dve.Fori(0, 2) as d:
                        n1, norm_write = d * NCH + (norm0 + NCH), affine(prm_m[:, 0:1], prm_m[:, 1:2])

                        def draining(t):
                            if t == DRAIN - 2:
                                dve.wait_ge(wm_in, (d + (2 * run + 1)) * 16)
                                norm_chunks(n1, norm_write, [0])

                        attention(run, d, draining)
                        norm_chunks(n1, norm_write, range(1, NCH))
                        mlp(run, d)
                    affines += 2 * NCH
                    need(dve, mlp_out, 2 * NCH * (run + 1))
                    for p0, p1, shift in halves:
                        last = STT(out=X[p0:p1, :], in0=YA[p0:p1, shift:shift + T], scalar=0.5, in1=X[p0:p1, :],
                                   op0=ALU.mult, op1=ALU.add)
                    last.then_inc(x_ffn, 1)
                elif kind == "S":
                    n_mid = [affines + 1 - (norm0 + NCH)]
                    norm_chunks(norm0 + NCH, affine(ln_gamma, ln_beta))
                    affines += NCH
                    ssm(norm0)
                elif kind == "M":
                    mixture(run)
                elif kind == "U":
                    unit()

        @block.gpsimd
        def _(pool):
            give_credit(pool, [rot_sum, halo])
            pool.wait_ge(cst_in, 16)
            for k, (kind, norm0, run) in enumerate(plan):
                ffns = sum(before == "F" for before, _, _ in plan[:k])
                if kind == "S":
                    if ffns:
                        need(pool, halo, HP * 2 * NCH * ffns)
                    pool.wait_ge(table_dve, 6)
                    wide = lambda v: v.unsqueeze(2).to_broadcast([L, 32, L])
                    for q in range(4):
                        nc.gpsimd.tensor_tensor(TG[L:P, 32 * q:32 * q + 32, :], wide(a_t[L:P, 32 * q:32 * q + 32]),
                                                decays[L:P].unsqueeze(1).to_broadcast([L, 32, L]), ALU.mult).then_inc(gt_prod, 1)
                    for q in range(4):
                        pool.wait_ge(gt_exp, q + 1)
                        v = TG[L:P, 32 * q:32 * q + 32, :]
                        nc.gpsimd.tensor_tensor(v, v, wide(cb_t[L:P, 32 * q:32 * q + 32]), ALU.mult).then_inc(gt_done, 1)
                if kind != "F":
                    continue
                if k:
                    x_whole(pool, k)
                nc.gpsimd.memset(KP, 0.0).then_inc(pool_init, 1)
                nc.gpsimd.memset(V, 0.0).then_inc(pool_init, 1)
                pool.wait_ge(pool_init, 3 * run + 2)
                nc.gpsimd.memset(V[:, :, :, DH:VW], 1.0).then_inc(pool_init, 1)
                with pool.Fori(0, 2) as d:
                    need(pool, s_mm, (d + 2 * run) * (NCH * 8))
                    zeros = zero_c.unsqueeze(2).to_broadcast([P, HP, WIN])
                    for e in range(2):
                        last = nc.gpsimd.tensor_tensor(KP[:, e, :, C:C + WIN], zeros, zeros, ALU.add)
                    last.then_inc(no_keys, 1)
                    with pool.Fori(0, NCH) as i:
                        g = d * NCH + i + 2 * NCH * run
                        pool.wait_ge(no_keys, d + (2 * run + 1))
                        for u in range(2 * HP):
                            need(pool, rotated, g * 8 + (u + 1))
                            nc.gpsimd.tensor_tensor(ta, ta, tb, ALU.add).then_inc(rot_sum, 1)
                            if u % 2:
                                nc.gpsimd.tensor_copy(KP[:, :, u // 2, 0:WIN], KP[:, :, u // 2, C:C + WIN]).then_inc(halo, 1)


def kernel(**inputs):
    from concourse.bacc import Bacc
    from concourse.bass_utils import run_bass_kernel_spmd

    a = {k: np.asarray(v) for k, v in inputs.items()}
    rot, mask, cst = shape_constants()
    col = lambda v: v.reshape(-1, 1)
    half = DH // 2

    wa, wm = [], []
    for l in range(2):
        wqkv, qs, ks = a["L0_ffn_wqkv"][l], a["L0_ffn_q_scale"][l], a["L0_ffn_k_scale"][l]
        turn = lambda s: np.concatenate([s[half:], s[:half]])
        twice = lambda s: col(np.concatenate([s, s]))
        wo = a["L0_ffn_wo"][l].reshape(HP, P, DM).transpose(1, 0, 2).reshape(P, HP * DM)
        wa.append(np.concatenate([wqkv, wo,
                                  twice(qs), twice(turn(qs)), twice(ks), twice(turn(ks))], 1))
        w2 = np.zeros((3 * P, DM), np.float32)
        w2[:HID] = a["L0_ffn_w2"][l]
        b1 = np.zeros((2, 3 * P), np.float32)
        b1[:, :HID] = a["L0_ffn_b1"][l].reshape(2, HID)
        wm.append(np.concatenate([a["L0_ffn_w1"][l], w2.reshape(3, P, DM).transpose(1, 0, 2).reshape(P, 3 * DM),
                                  col(a["L0_ffn_ln_g"][l]), col(a["L0_ffn_ln_b"][l]), b1.reshape(6, P).T,
                                  col(a["L0_ffn_b2"][l])], 1))

    def by_state(v):
        return np.concatenate([v.T, v.T], 0)

    la, b_, c_ = a["L0_attn_log_A"], a["L0_attn_B_param"], a["L0_attn_C_param"]
    ssm = np.concatenate([la, b_, c_, col(a["L0_attn_log_dt"]), col(a["L0_attn_D_param"]), col(a["L0_attn_ln_gamma"]),
                          col(a["L0_attn_ln_beta"]), col(a["L0_attn_b_out"]),
                          by_state(la), by_state(b_), by_state(c_),
                          np.tile(a["L0_attn_log_dt"][None, :], (P, 1)), a["L0_attn_W_out"].T], 1)
    uw, vw, ow = a["L1_attn_u_w"], a["L1_attn_v_w"], a["L1_attn_o_w"]
    heads_t0 = np.repeat(a["L1_attn_t_zero"][:, 0], 256 // HEADS)
    unit = np.concatenate([uw.T, vw.T, ow.T.reshape(2, P, DM).transpose(1, 0, 2).reshape(P, 2 * DM),
                           a["L1_attn_u_b"].reshape(2, P).T, a["L1_attn_v_b"].reshape(2, P).T,
                           heads_t0.reshape(2, P).T, col(a["L1_attn_o_b"])], 1)
    arrays = {
        "x": a["L0_attn_x"][0].T, "rot": rot, "mask": mask, "cst": cst, "wa": np.stack(wa + wa[:1]), "wm": np.stack(wm + wm[:1]),
        "ssm": ssm, "log_a_row": la.reshape(1, -1), "unit": unit,
        "mw1": a["L1_ffn_w1"].transpose(1, 0, 2),
        "mw2": a["L1_ffn_w2"].reshape(NE, MB, P, DM).transpose(2, 0, 1, 3),
        "mb1": a["L1_ffn_b1"].reshape(NE, MB, P).transpose(2, 0, 1).reshape(P, NE * MB),
        "mb2": a["L1_ffn_b2"].reshape(1, NE * DM), "mwr": a["L1_ffn_w_router"],
    }
    arrays = {f"in_{k}": np.ascontiguousarray(v) for k, v in arrays.items()}
    nc = Bacc("TRN2", target_bir_lowering=False, num_devices=1)
    ins = {k[3:]: nc.dram_tensor(k, v.shape, F32, kind="ExternalInput").ap() for k, v in arrays.items()}
    out = nc.dram_tensor("out_0", (DM, T), F32, kind="ExternalOutput").ap()
    macaron_kernel(nc, ins, out)
    r = run_bass_kernel_spmd(nc, [arrays], core_ids=[0])
    return np.ascontiguousarray(r.results[0]["out_0"].T).reshape(1, T, DM)
```
